# Optimizing a Trainium2 kernel written in Bass

```python
import numpy as np
import jax
import jax.numpy as jnp

def _softmax(x, axis=-1):
    return jax.nn.softmax(x, axis=axis)

def _gelu(x):
    return jax.nn.gelu(x, approximate=True)

def _silu(x):
    return jax.nn.silu(x)

def _sigmoid(x):
    return jax.nn.sigmoid(x)

def _layernorm(x, axis=-1, eps=1e-05):
    m = jnp.mean(x, axis=axis, keepdims=True)
    v = jnp.var(x, axis=axis, keepdims=True)
    return (x - m) / jnp.sqrt(v + eps)

def _scatter_add(tgt, idx, src, axis=0):
    return tgt.at[idx].add(src)

def _segment_sum(src, seg, n):
    return jax.ops.segment_sum(src, seg, n)
kernel_name = 'mk_gnn_ffn_d1_gnn_r8_cb85c2'

def setup_inputs(seed: int=0):
    np.random.seed(seed)
    _w = jnp.asarray

    def _rec_inputs():
        import jax
        import jax.numpy as jnp
        _gk = jax.random.key(seed)
        x = -0.0005963 + 1.001 * jax.random.normal(jax.random.fold_in(_gk, 1), (384, 1024), jnp.float32)
        src = jax.random.randint(jax.random.fold_in(_gk, 2), (6144,), 0, 384, jnp.int32)
        dst = jax.random.randint(jax.random.fold_in(_gk, 3), (6144,), 0, 384, jnp.int32)
        _o = jnp.argsort(dst, stable=True)
        src = src[_o]
        dst = dst[_o]
        edge_type_5 = jax.random.randint(jax.random.fold_in(_gk, 12), (6144,), 0, 5, jnp.int32)
        return (x, src, dst, edge_type_5)
    x, src, dst, edge_type_5 = _rec_inputs()

    def _L0_gnn_setup():
        import jax, jax.numpy as jnp
        import numpy as np
        N = 384
        E = 12288
        IN_F = 1024
        OUT_F = 1024
        H = 16
        D = OUT_F // H
        NUM_ETYPES = 4

        def _build_mask(edge_index, edge_type, edge_type_weights, dtype):
            src, dst = (edge_index[0], edge_index[1])
            w = jax.nn.softplus(edge_type_weights)
            mask = jnp.full((N, N), -jnp.inf, dtype=dtype)
            mask = mask.at[src, dst].set(w[edge_type - 1])
            diag = jnp.diagonal(mask)
            idx = jnp.arange(N)
            mask = mask.at[idx, idx].set(jnp.where(jnp.isneginf(diag), w[3], diag))
            return mask
        key = jax.random.key(seed)
        ks = jax.random.split(key, 20)
        p = lambda k, shape: jax.random.normal(k, shape, dtype=jnp.float32) * 0.02
        return {'x': jax.random.normal(ks[0], (N, IN_F), dtype=jnp.float32), 'edge_index': jax.random.randint(ks[1], (2, E), 0, N), 'edge_type': jax.random.randint(ks[2], (E,), 1, NUM_ETYPES + 1), 'edge_type_weights': jnp.ones((NUM_ETYPES,), jnp.float32) + 0.1 * jax.random.normal(ks[3], (NUM_ETYPES,), dtype=jnp.float32), 'wq': p(ks[4], (OUT_F, IN_F)), 'bq': p(ks[5], (OUT_F,)), 'wk': p(ks[6], (OUT_F, IN_F)), 'bk': p(ks[7], (OUT_F,)), 'wv': p(ks[8], (OUT_F, IN_F)), 'bv': p(ks[9], (OUT_F,)), 'wiq': p(ks[10], (OUT_F, OUT_F)), 'biq': p(ks[11], (OUT_F,)), 'wik': p(ks[12], (OUT_F, OUT_F)), 'bik': p(ks[13], (OUT_F,)), 'wiv': p(ks[14], (OUT_F, OUT_F)), 'biv': p(ks[15], (OUT_F,)), 'wo': p(ks[16], (OUT_F, OUT_F)), 'bo': p(ks[17], (OUT_F,))}
    _L0_gnn_all = _L0_gnn_setup()
    _L0_gnn_in = {k: v for k, v in _L0_gnn_all.items() if k in ('edge_type_weights', 'wq', 'bq', 'wk', 'bk', 'wv', 'bv', 'wiq', 'biq', 'wik', 'bik', 'wiv', 'biv', 'wo', 'bo')}
    del _L0_gnn_all

    def _L0_ffn_setup():
        import jax, jax.numpy as jnp
        import numpy as np
        B, S, D = (2, 256, 1024)
        H, E, P, K = (8, 8, 128, 2)
        SCALE = 1.0 / np.sqrt(P)

        def _get_sel_gate(x, w, route_scale):
            logits = jnp.einsum('bsd,ed->bse', x, w).astype(jnp.float32)
            raw = logits.reshape(x.shape[0], x.shape[1], H, E)
            probs = jax.nn.sigmoid(raw)
            vals, idx = jax.lax.top_k(probs, K)
            vals = vals / jnp.clip(vals.sum(-1, keepdims=True), 1e-09)
            vals = vals * route_scale
            gate = (jax.nn.one_hot(idx, E, dtype=vals.dtype) * vals[..., None]).sum(-2)
            return gate
        key = jax.random.key(seed)
        ks = jax.random.split(key, 8)
        std = 1.0 / np.sqrt(D)
        return {'x': jax.random.normal(ks[0], (B, S, D), jnp.float32), 'q_w': jax.random.normal(ks[1], (H * P, D), jnp.float32) * std, 'k_w': jax.random.normal(ks[2], (H * P, D), jnp.float32) * std, 'v_w': jax.random.normal(ks[3], (H * E, D, P), jnp.float32) * std, 'o_w': jax.random.normal(ks[4], (H * E, P, D), jnp.float32) * (1.0 / np.sqrt(H * P)), 'sel_v_w': jax.random.normal(ks[5], (H * E, D), jnp.float32) * std, 'sel_o_w': jax.random.normal(ks[6], (H * E, D), jnp.float32) * std, 'route_scale': jnp.ones((1,), jnp.float32)}
    _L0_ffn_all = _L0_ffn_setup()
    _L0_ffn_in = {k: v for k, v in _L0_ffn_all.items() if k in ('q_w', 'k_w', 'v_w', 'o_w', 'sel_v_w', 'sel_o_w', 'route_scale')}
    del _L0_ffn_all
    return {'x': x, 'src': src, 'dst': dst, 'edge_type_5': edge_type_5, 'L0_gnn_edge_type_weights': _L0_gnn_in['edge_type_weights'], 'L0_gnn_wq': _L0_gnn_in['wq'], 'L0_gnn_bq': _L0_gnn_in['bq'], 'L0_gnn_wk': _L0_gnn_in['wk'], 'L0_gnn_bk': _L0_gnn_in['bk'], 'L0_gnn_wv': _L0_gnn_in['wv'], 'L0_gnn_bv': _L0_gnn_in['bv'], 'L0_gnn_wiq': _L0_gnn_in['wiq'], 'L0_gnn_biq': _L0_gnn_in['biq'], 'L0_gnn_wik': _L0_gnn_in['wik'], 'L0_gnn_bik': _L0_gnn_in['bik'], 'L0_gnn_wiv': _L0_gnn_in['wiv'], 'L0_gnn_biv': _L0_gnn_in['biv'], 'L0_gnn_wo': _L0_gnn_in['wo'], 'L0_gnn_bo': _L0_gnn_in['bo'], 'L0_ffn_q_w': _L0_ffn_in['q_w'], 'L0_ffn_k_w': _L0_ffn_in['k_w'], 'L0_ffn_v_w': _L0_ffn_in['v_w'], 'L0_ffn_o_w': _L0_ffn_in['o_w'], 'L0_ffn_sel_v_w': _L0_ffn_in['sel_v_w'], 'L0_ffn_sel_o_w': _L0_ffn_in['sel_o_w'], 'L0_ffn_route_scale': _L0_ffn_in['route_scale']}

def reference(x, src, dst, edge_type_5, L0_gnn_edge_type_weights, L0_gnn_wq, L0_gnn_bq, L0_gnn_wk, L0_gnn_bk, L0_gnn_wv, L0_gnn_bv, L0_gnn_wiq, L0_gnn_biq, L0_gnn_wik, L0_gnn_bik, L0_gnn_wiv, L0_gnn_biv, L0_gnn_wo, L0_gnn_bo, L0_ffn_q_w, L0_ffn_k_w, L0_ffn_v_w, L0_ffn_o_w, L0_ffn_sel_v_w, L0_ffn_sel_o_w, L0_ffn_route_scale):
    import jax
    import jax.numpy as jnp

    def _L0_gnn_ref(x, edge_index, edge_type, edge_type_weights, wq, bq, wk, bk, wv, bv, wiq, biq, wik, bik, wiv, biv, wo, bo):
        import jax, jax.numpy as jnp
        import numpy as np
        N = 384
        E = 12288
        IN_F = 1024
        OUT_F = 1024
        H = 16
        D = OUT_F // H
        NUM_ETYPES = 4

        def _build_mask(edge_index, edge_type, edge_type_weights, dtype):
            src, dst = (edge_index[0], edge_index[1])
            w = jax.nn.softplus(edge_type_weights)
            mask = jnp.full((N, N), -jnp.inf, dtype=dtype)
            mask = mask.at[src, dst].set(w[edge_type - 1])
            diag = jnp.diagonal(mask)
            idx = jnp.arange(N)
            mask = mask.at[idx, idx].set(jnp.where(jnp.isneginf(diag), w[3], diag))
            return mask
        q = x @ wq.T + bq
        k = x @ wk.T + bk
        v = x @ wv.T + bv
        q2 = (q @ wiq.T + biq).reshape(N, H, D).transpose(1, 0, 2)
        k2 = (k @ wik.T + bik).reshape(N, H, D).transpose(1, 0, 2)
        v2 = (v @ wiv.T + biv).reshape(N, H, D).transpose(1, 0, 2)
        mask = _build_mask(edge_index, edge_type, edge_type_weights, x.dtype)
        scale = 1.0 / np.sqrt(D).astype(np.float32)
        scores = jnp.einsum('hnd,hmd->hnm', q2, k2) * scale + mask[None]
        attn = jax.nn.softmax(scores, axis=-1)
        out = jnp.einsum('hnm,hmd->hnd', attn, v2)
        out = out.transpose(1, 0, 2).reshape(N, OUT_F)
        return out @ wo.T + bo

    def _L0_ffn_ref(x, q_w, k_w, v_w, o_w, sel_v_w, sel_o_w, route_scale):
        import jax, jax.numpy as jnp
        import numpy as np
        B, S, D = (2, 256, 1024)
        H, E, P, K = (8, 8, 128, 2)
        SCALE = 1.0 / np.sqrt(P)

        def _get_sel_gate(x, w, route_scale):
            logits = jnp.einsum('bsd,ed->bse', x, w).astype(jnp.float32)
            raw = logits.reshape(x.shape[0], x.shape[1], H, E)
            probs = jax.nn.sigmoid(raw)
            vals, idx = jax.lax.top_k(probs, K)
            vals = vals / jnp.clip(vals.sum(-1, keepdims=True), 1e-09)
            vals = vals * route_scale
            gate = (jax.nn.one_hot(idx, E, dtype=vals.dtype) * vals[..., None]).sum(-2)
            return gate
        rs = route_scale[0]
        gate_v = _get_sel_gate(x, sel_v_w, rs)
        gate_o = _get_sel_gate(x, sel_o_w, rs)
        q = jnp.einsum('bsd,hpd->bhsp', x, q_w.reshape(H, P, D))
        k = jnp.einsum('bsd,hpd->bhsp', x, k_w.reshape(H, P, D))
        xv = jnp.einsum('bsd,hedp->bshep', x, v_w.reshape(H, E, D, P))
        v = jnp.einsum('bshep,bshe->bhsp', xv, gate_v)
        att = jax.nn.softmax(jnp.einsum('bhqp,bhkp->bhqk', q, k) * SCALE, axis=-1)
        ctx = jnp.einsum('bhqk,bhkp->bqhp', att, v)
        weighted = ctx[:, :, :, None, :] * gate_o[..., None]
        out = jnp.einsum('bshep,hepd->bsd', weighted, o_w.reshape(H, E, P, D))
        return out
    edge_index = jnp.stack([src, dst])
    x = x + _L0_gnn_ref(_layernorm(x, axis=-1), edge_index, edge_type_5, L0_gnn_edge_type_weights, L0_gnn_wq, L0_gnn_bq, L0_gnn_wk, L0_gnn_bk, L0_gnn_wv, L0_gnn_bv, L0_gnn_wiq, L0_gnn_biq, L0_gnn_wik, L0_gnn_bik, L0_gnn_wiv, L0_gnn_biv, L0_gnn_wo, L0_gnn_bo)
    x = x + _L0_ffn_ref(_layernorm(x, axis=-1)[None], L0_ffn_q_w, L0_ffn_k_w, L0_ffn_v_w, L0_ffn_o_w, L0_ffn_sel_v_w, L0_ffn_sel_o_w, L0_ffn_route_scale)[0]
    return x

_drawn_inputs = setup_inputs


def setup_inputs(seed=0):
    import zlib

    import numpy as np

    out = dict(_drawn_inputs(seed))
    spreads = {}
    factors = {'L0_gnn_edge_type_weights': 5.419,
     'L0_gnn_wq': 3.821,
     'L0_gnn_bq': 8.0,
     'L0_gnn_wk': 3.618,
     'L0_gnn_bk': 8.0,
     'L0_gnn_bv': 4.381,
     'L0_gnn_wiq': 3.536,
     'L0_gnn_biq': 8.0,
     'L0_gnn_wik': 3.309,
     'L0_gnn_bik': 8.0,
     'L0_gnn_biv': 3.586}
    for name, (base, spread) in spreads.items():
        noise = np.random.default_rng([zlib.crc32(name.encode()), seed]).standard_normal(out[name].shape)
        drawn = base * np.exp(spread * noise) if base else spread * noise
        out[name] = jnp.asarray(drawn.astype(out[name].dtype))
    for name, factor in factors.items():
        out[name] = (out[name] * factor).astype(out[name].dtype)
    return out
```

```python
import concourse.bass as bass
from concourse import mybir
from contextlib import ExitStack


P = 128
N = 384
NT = N // P
D = 1024
KT = D // P
HALF = D // 2
EDGES = 6144
CHUNKS = EDGES // P
GD = 64
PAIRS = D // P
FH = 8
FE = 8
GROUPS = 2 * FH
EPS = 1e-5
GNN_SCALE = 1.0 / 8.0
FFN_SCALE = float(P) ** -0.5
NO_EDGE = -(2.0 ** 120)

RING = 3
U_PAIR = 3 * PAIRS
U_WO = U_PAIR + 3 * PAIRS
U_ROUTER = U_WO + 8
U_HEAD = U_ROUTER + 1
HEAD_UNITS = 10
BODY_UNITS = 18
U_LOOP = U_HEAD + HEAD_UNITS
U_LAST = U_LOOP + (FH - 1) * BODY_UNITS
UNITS = U_LAST + 8
assert UNITS % RING == 0 and U_ROUTER % RING == 2 and BODY_UNITS % RING == 0

LN_BANKS = (6, 7, 0, 1)
RF = 5
QF, KF = 0, 1
VF = ((2, 3, 4), (0, 1, 2))
SF = (5, 6, 7)
TF = (0, 1, 2)
OF = ((3, 4, 5), (6, 7, 3))
CF = 4
PIECE = CHUNKS // PAIRS


class Tally:

    def __init__(self, sem):
        self.sem, self.n, self.turns = sem, 0, 0

    def add(self, instruction):
        instruction.then_inc(self.sem, 1)
        self.n += 1

    def value(self):
        return self.turns + self.n

    def enter(self, turn, per_turn):
        self.start, self.per_turn = self.n, per_turn
        self.turns = turn * per_turn

    def leave(self, turns):
        assert self.n - self.start == self.per_turn, (self.n - self.start, self.per_turn)
        self.n, self.turns = self.start + self.per_turn * turns, 0


def gnn_switch_kernel(nc, x_in, units, biases, bo, edge_type_weights, route_scale, edge_cols, src_row, dst_row, out):
    fp32, f32r, bf16 = mybir.dt.float32, mybir.dt.float32r, mybir.dt.bfloat16
    fp16, int32 = mybir.dt.float16, mybir.dt.int32
    ALU, ACT, AX = mybir.AluOpType, mybir.ActivationFunctionType, mybir.AxisListType.X

    ctx = ExitStack()
    with ctx:
        def sb(name, shape, dt):
            return ctx.enter_context(nc.sbuf_tensor(name, shape, dt))

        def sem(name):
            return ctx.enter_context(nc.semaphore(name))

        w_raw = sb("w_raw", [P, RING, D], fp32)
        w_hi = sb("w_hi", [P, RING, D], f32r)
        w_lo = sb("w_lo", [P, RING, D], f32r)
        hT_hi, hT_lo = sb("hT_hi", [P, KT, N], f32r), sb("hT_lo", [P, KT, N], f32r)
        qT_hi, qT_lo = sb("qT_hi", [P, KT, N], f32r), sb("qT_lo", [P, KT, N], f32r)
        kT_hi, kT_lo = sb("kT_hi", [P, KT, N], f32r), sb("kT_lo", [P, KT, N], f32r)
        vT_hi, vT_lo = sb("vT_hi", [P, KT, N], f32r), sb("vT_lo", [P, KT, N], f32r)
        oT_hi, oT_lo = hT_hi, hT_lo
        gc_hi, gc_lo = qT_hi, qT_lo
        q2_hi, q2_lo = sb("q2_hi", [P, N], f32r), sb("q2_lo", [P, N], f32r)
        k2_hi, k2_lo = sb("k2_hi", [P, N], f32r), sb("k2_lo", [P, N], f32r)
        v2_hi, v2_lo = sb("v2_hi", [P, NT, 2 * P], f32r), sb("v2_lo", [P, NT, 2 * P], f32r)
        pT_hi, pT_lo = sb("pT_hi", [P, NT, N], f32r), sb("pT_lo", [P, NT, N], f32r)
        x = sb("x", [P, NT, D], fp32)
        mask8 = sb("mask8", [P, NT, N], fp32)
        v2T = sb("v2T", [P, N], fp32)
        gates = sb("gates", [P, NT, GROUPS * FE], fp32)
        scratch = sb("scratch", [P, 6144], fp32)
        normed = scratch[:, 3072:6144].rearrange("p (t d) -> p t d", t=NT)
        rows = scratch[:, 0:2 * PIECE * P].bitcast(int32).rearrange("p (a n) -> p a n", a=2)
        keys = scratch[:, 1536:1536 + PIECE * P].rearrange("p (c q) -> p c q", c=PIECE)
        hot = scratch[:, 3072:3072 + PIECE * N].bitcast(bf16).rearrange("p (a c n) -> p a c n", a=2, c=PIECE)
        counts = scratch[:, 0:NT * N].rearrange("p (t n) -> p t n", t=NT)
        types = scratch[:, 1152:2304].bitcast(int32)
        picked = scratch[:, 2304:3456]
        S = scratch[:, 0:6 * N].rearrange("p (t n) -> p t n", t=6)
        route = scratch[:, 0:3072].rearrange("p (a g e) -> p a g e", a=8, e=FE)
        gate_rows = scratch[:, 0:3072].rearrange("p (e n) -> p e n", e=FE)
        F = scratch[:, 3072:3072 + NT * N].rearrange("p (t n) -> p t n", t=NT)
        gated = scratch[:, 4224:4224 + 2 * N].rearrange("p (b n) -> p b n", b=2)
        context = scratch[:, 4992:4992 + N]
        v_sum = scratch[:, 5376:5376 + N].rearrange("p (t d) -> p t d", t=NT)
        gateT = scratch[0:FH * FE, 5760:5760 + N]
        iota_i = sb("iota_i", [P, N], int32)
        iota = sb("iota", [P, N], fp16)
        ident = sb("ident", [P, P], fp32)
        later = sb("later", [P, P], fp32)
        eye_wide = sb("eye_wide", [P, 5 * P], bf16)
        eye_self = sb("eye_self", [P, P], bf16)
        desc = sb("desc", [P, FE], fp32)
        chunk_base = sb("chunk_base", [P, CHUNKS], int32)
        bias = sb("bias", [P, 6, KT], fp32)
        edge = sb("edge", [P, 3, CHUNKS], int32)
        table = sb("table", [P, CHUNKS, 4], fp32)
        now = sb("now", [P, PIECE, 4], fp32)
        dup = sb("dup", [P, PIECE], fp32)
        weight = sb("weight", [P, PIECE], fp32)
        code = sb("code", [P, CHUNKS], int32)
        etw = sb("etw", [P, 4], fp32)
        etw_abs = sb("etw_abs", [P, 4], fp32)
        w8 = sb("w8", [P, 4], fp32)
        rs = sb("rs", [P, 1], fp32)
        stats = sb("stats", [P, NT, 2, 6], fp32)
        moments = sb("moments", [P, NT, 2], fp32)
        var_eps = sb("var_eps", [P, NT], fp32)
        minus_half = sb("minus_half", [P, NT], fp32)
        rstd = sb("rstd", [P, NT], fp32)
        mx = sb("mx", [P, 6], fp32)
        neg_mx = sb("neg_mx", [P, 6], fp32)
        row_sum = sb("row_sum", [P, 6], fp32)
        inv_sum = sb("inv_sum", [P, 6], fp32)
        holds = sb("holds", [P, 6], fp32)
        best = sb("best", [P, 6, 3 * GROUPS], fp32)
        v_gate = sb("v_gate", [P, NT, FE], fp32)

        bank = [ctx.enter_context(nc.psum_tensor(f"bank{i}", [P, 512], fp32)) for i in range(8)]
        gate_rows_dram = nc.dram_tensor("gate_rows_scratch", (FH * FE, N), fp32).ap()

        raw_landed = [sem(f"raw_landed{s}") for s in range(RING)]
        hi_ready, lo_ready, unit_used = sem("hi_ready"), sem("lo_ready"), sem("unit_used")
        x_landed = [sem(f"x_landed{t}") for t in range(NT)]
        consts_landed, bo_landed = sem("consts_landed"), sem("bo_landed")
        pool_consts, pool_step, dve_consts = sem("pool_consts"), sem("pool_step"), sem("dve_consts")
        var_ready, rstd_ready, normed_ready = sem("var_ready"), sem("rstd_ready"), sem("normed_ready")
        normed_T, hT_hi_done, hT_lo_done = sem("normed_T"), sem("hT_hi_done"), sem("hT_lo_done")
        qkv_hi_done, qkv_lo_done = sem("qkv_hi_done"), sem("qkv_lo_done")
        rows_landed, keys_made = sem("rows_landed"), sem("keys_made")
        hot_ready, hot_used, counts_done = sem("hot_ready"), sem("hot_used"), sem("counts_done")
        etw_abs_ready, etw_exp, etw_exp1, etw_log = (sem("etw_abs_ready"), sem("etw_exp"), sem("etw_exp1"),
                                                     sem("etw_log"))
        v2_cleared, mask_ready, dve_step = sem("v2_cleared"), sem("mask_ready"), sem("dve_step")
        q2_hi_done, q2_lo_done, k2_hi_done, k2_lo_done = (sem("q2_hi_done"), sem("q2_lo_done"), sem("k2_hi_done"),
                                                          sem("k2_lo_done"))
        v2T_ready, v2_back, v2_hi_done, v2_lo_done = (sem("v2T_ready"), sem("v2_back"), sem("v2_hi_done"),
                                                      sem("v2_lo_done"))
        scores_done, max_ready, exp_done, norm_done = (sem("scores_done"), sem("max_ready"), sem("exp_done"),
                                                       sem("norm_done"))
        probs_T, pT_hi_done, pT_lo_done = sem("probs_T"), sem("pT_hi_done"), sem("pT_lo_done")
        pair_out_first, pair_out = sem("pair_out_first"), sem("pair_out")
        oT_hi_done, oT_lo_done, bo_added = sem("oT_hi_done"), sem("oT_lo_done"), sem("bo_added")
        router_exp, gates_ready, gates_T, gateT_ready = (sem("router_exp"), sem("gates_ready"), sem("gates_T"),
                                                         sem("gateT_ready"))
        gates_stored, rows_ready = sem("gates_stored"), sem("rows_ready")
        fq_hi_done, fq_lo_done, fk_hi_done, fk_lo_done = (sem("fq_hi_done"), sem("fq_lo_done"), sem("fk_hi_done"),
                                                          sem("fk_lo_done"))
        v_gated, fv_hi_done, fv_lo_done = sem("v_gated"), sem("fv_hi_done"), sem("fv_lo_done")
        f_scores, f_max, f_exp, f_norm = sem("f_scores"), sem("f_max"), sem("f_exp"), sem("f_norm")
        f_probs_T, f_pT_hi, f_pT_lo = sem("f_probs_T"), sem("f_pT_hi"), sem("f_pT_lo")
        f_context, context_ready = sem("f_context"), sem("context_ready")
        gated_ready, gc_hi_done, gc_lo_done, out_added = (sem("gated_ready"), sem("gc_hi_done"), sem("gc_lo_done"),
                                                          sem("out_added"))
        out_stored = sem("out_stored")

        bo_row = scratch[:, 0:D]

        x_tiles = x_in.rearrange("(t p) d -> p t d", p=P)
        out_tiles = out.rearrange("(t p) d -> p t d", p=P)

        block = ctx.enter_context(nc.Block())

        @block.sync
        def _(sp):
            for t in range(NT):
                sp.dma_start(x[:, t, :], x_tiles[:, t, :]).then_inc(x_landed[t], 16)
            for s in range(RING):
                sp.dma_start(w_raw[:, s, :], units[s]).then_inc(raw_landed[s], 16)
            with sp.Fori(1, UNITS // RING) as turn:
                for s in range(RING):
                    sp.wait_ge(lo_ready, turn * RING + (s - RING + 1))
                    sp.dma_start(w_raw[:, s, :], units[turn * RING + s]).then_inc(raw_landed[s], 16)
            for f in range(2):
                for t in range(NT):
                    sp.wait_ge(out_added, 6 * FH + NT * f + t + 1)
                    sp.dma_start(out_tiles[:, t, f * HALF:(f + 1) * HALF],
                                 x[:, t, f * HALF:(f + 1) * HALF]).then_inc(out_stored, 16)
            sp.wait_ge(out_stored, 16 * 2 * NT)

        @block.gpsimd
        def _(pool):
            pool.memset(minus_half[:], -0.5).then_inc(pool_consts, 1)
            pool.memset(ident[:], 0.0).then_inc(pool_step, 1)
            pool.wait_ge(pool_step, 1)
            pool.affine_select(out=ident[:], in_=ident[:], compare_op=ALU.not_equal, fill=1.0, base=0,
                               pattern=[[-1, P]], channel_multiplier=1).then_inc(pool_consts, 1)

            def rstd_of():
                pool.tensor_tensor(rstd[:], var_eps[:], minus_half[:], ALU.pow).then_inc(rstd_ready, 1)

            def make_lo(u, s):
                pool.wait_ge(hi_ready, u + 1)
                pool.tensor_tensor(w_lo[:, s, :], w_raw[:, s, :], w_hi[:, s, :].bitcast(fp32),
                                   ALU.subtract).then_inc(lo_ready, 1)

            pool.memset(later[:], 1.0).then_inc(pool_step, 1)
            pool.wait_ge(pool_step, 2)
            pool.affine_select(out=later[:], in_=later[:], compare_op=ALU.is_gt, fill=0.0, base=0,
                               pattern=[[1, P]], channel_multiplier=-1).then_inc(pool_consts, 1)
            pool.iota(iota_i[:], pattern=[[1, N]], base=0, channel_multiplier=0).then_inc(pool_consts, 1)
            pool.iota(chunk_base[:], pattern=[[4, CHUNKS]], base=32, channel_multiplier=0).then_inc(pool_consts, 1)
            for e in range(FE):
                pool.memset(desc[:, e:e + 1], float(FE - e)).then_inc(pool_consts, 1)
            pool.memset(eye_wide[:], 0.0).then_inc(pool_step, 1)
            pool.memset(eye_self[:], 0.0).then_inc(pool_step, 1)
            pool.wait_ge(pool_step, 4)
            pool.affine_select(out=eye_wide[:], in_=eye_wide[:], compare_op=ALU.not_equal, fill=1.0, base=2 * P,
                               pattern=[[-1, 5 * P]], channel_multiplier=1).then_inc(pool_consts, 1)
            pool.affine_select(out=eye_self[:], in_=eye_self[:], compare_op=ALU.not_equal, fill=2.0 ** (30 - 127),
                               base=0, pattern=[[-1, P]], channel_multiplier=1).then_inc(pool_consts, 1)
            pool.wait_ge(var_ready, 1)
            pool.wait_ge(pool_consts, 1)
            rstd_of()
            with pool.Fori(0, U_HEAD // RING) as turn:
                for s in range(RING):
                    make_lo(turn * RING + s, s)
            pool.wait_ge(var_ready, 2)
            rstd_of()
            with pool.Fori(U_HEAD // RING, UNITS // RING) as turn:
                for s in range(RING):
                    make_lo(turn * RING + s, s)

        @block.scalar
        def _(act):
            n_consts = 0
            for dst, src in ((bias[:], biases), (edge[:], edge_cols),
                             (etw[:], edge_type_weights.partition_broadcast(P)),
                             (rs[:], route_scale.partition_broadcast(P))):
                act.dma_start(dst, src).then_inc(consts_landed, 16)
                n_consts += 1
            act.dma_start(bo_row, bo.partition_broadcast(P)).then_inc(bo_landed, 16)

            def hi_at(base, step, per):
                first, turn = base
                u = first + step
                s = u % RING
                landed = 16 * (u // RING + 1)
                act.wait_ge(raw_landed[s], turn * (16 * per // RING) + landed)
                act.wait_ge(unit_used, turn * per + (u - (RING - 1)))
                act.activation(w_hi[:, s, :], w_raw[:, s, :], ACT.Copy).then_inc(hi_ready, 1)

            def hi_fixed(u, fresh=False):
                s = u % RING
                act.wait_ge(raw_landed[s], 16 * (u // RING + 1))
                if not fresh:
                    act.wait_ge(unit_used, u - (RING - 1))
                act.activation(w_hi[:, s, :], w_raw[:, s, :], ACT.Copy).then_inc(hi_ready, 1)

            def hT_his(base):
                for k in range(KT):
                    act.wait_ge(normed_T, base + k + 1)
                    act.activation(hT_hi[:, k, :], bank[LN_BANKS[k % 4]][:, 0:N], ACT.Copy).then_inc(hT_hi_done, 1)

            act.wait_ge(etw_abs_ready, 1)
            act.activation(w8[:], etw_abs[:], ACT.Exp, scale=-1.0).then_inc(etw_exp, 1)
            act.wait_ge(etw_exp1, 1)
            act.activation(etw_abs[:], w8[:], ACT.Ln).then_inc(etw_log, 1)
            hi_fixed(0, fresh=True)
            hi_fixed(1, fresh=True)
            hi_fixed(2, fresh=True)
            hT_his(0)

            def load_rows(piece_words):
                act.dma_start(rows[:, 0, :], src_row[piece_words].partition_broadcast(P)).then_inc(rows_landed, 16)
                act.dma_start(rows[:, 1, :], dst_row[piece_words].partition_broadcast(P)).then_inc(rows_landed, 16)

            act.wait_ge(bo_added, 1)
            load_rows(0)
            with act.Fori(0, PAIRS) as j:
                for i, dst in enumerate((qT_hi, kT_hi, vT_hi)):
                    act.wait_ge(unit_used, j * 3 + i + 1)
                    act.activation(dst[:, j, :], bank[i][:, 0:N], ACT.Identity,
                                   bias=bias[:, i, bass.ds(j, 1)]).then_inc(qkv_hi_done, 1)
                    hi_at((0, j), i + 3, 3)
                act.wait_ge(keys_made, j + 1)
                load_rows(j + 1)

            def q2_hi_of(turn, b):
                act.wait_ge(unit_used, U_PAIR + 1 + turn * 3)
                act.activation(q2_hi[:], bank[6][:, 0:N], ACT.Identity, bias=b).then_inc(q2_hi_done, 1)

            def k2_hi_of(turn, b):
                act.wait_ge(unit_used, U_PAIR + 2 + turn * 3)
                act.activation(k2_hi[:], bank[6][:, 0:N], ACT.Identity, bias=b).then_inc(k2_hi_done, 1)

            def v2_hi_of(pair):
                act.wait_ge(v2_back, pair + 1)
                act.activation(v2_hi.rearrange("p t (a d) -> p t a d", a=2)[:, :, :, 0:GD],
                               bank[7][:, 0:N].rearrange("p (t a d) -> p t a d", t=NT, a=2),
                               ACT.Copy).then_inc(v2_hi_done, 1)

            def pT_hi_of(pair, head):
                for m in range(NT):
                    act.wait_ge(probs_T, pair * 6 + NT * head + m + 1)
                    if head and m == 0:
                        act.wait_ge(pair_out_first, pair + 1)
                    act.activation(pT_hi[:, m, :], bank[NT * head + m][:, 0:N], ACT.Copy).then_inc(pT_hi_done, 1)

            def exp_of(pair, head):
                act.wait_ge(max_ready, pair * 2 + head + 1)
                for t in range(NT):
                    c = NT * head + t
                    act.activation(S[:, c, :], S[:, c, :], ACT.Exp, bias=neg_mx[:, c:c + 1],
                                   accum_out=row_sum[:, c:c + 1]).then_inc(exp_done, 1)

            def oT_hi_of(pair, at):
                act.wait_ge(pair_out, pair + 1)
                act.activation(oT_hi[:, at, :], bank[7][:, 0:N], ACT.Copy).then_inc(oT_hi_done, 1)

            q2_hi_of(0, bias[:, 3, 0:1])
            hi_fixed(U_PAIR + 3)
            k2_hi_of(0, bias[:, 4, 0:1])
            hi_fixed(U_PAIR + 4)
            exp_of(0, 0)
            exp_of(0, 1)
            with act.Fori(1, PAIRS) as j:
                hi_at((U_PAIR, j), 2, 3)
                q2_hi_of(j, bias[:, 3, bass.ds(j, 1)])
                v2_hi_of(j - 1)
                pT_hi_of(j - 1, 0)
                hi_at((U_PAIR, j), 3, 3)
                k2_hi_of(j, bias[:, 4, bass.ds(j, 1)])
                hi_at((U_PAIR, j), 4, 3)
                pT_hi_of(j - 1, 1)
                oT_hi_of(j - 1, j - 1)
                exp_of(j, 0)
                exp_of(j, 1)
            hi_fixed(U_WO + 2)
            v2_hi_of(PAIRS - 1)
            pT_hi_of(PAIRS - 1, 0)
            pT_hi_of(PAIRS - 1, 1)
            oT_hi_of(PAIRS - 1, PAIRS - 1)
            for u in range(U_WO + 3, U_ROUTER + 3):
                hi_fixed(u)
            hT_his(KT)
            act.wait_ge(unit_used, U_ROUTER + 1)
            act.activation(route[:, 0].rearrange("p g e -> p (g e)"), bank[RF][:, 0:N], ACT.Exp,
                           scale=-1.0).then_inc(router_exp, 1)

            def f_hi_of(dst, b, done, need):
                act.wait_ge(unit_used, need)
                act.activation(dst[:], bank[b][:, 0:N], ACT.Copy).then_inc(done, 1)

            def f_exp_of(head):
                for t in range(NT):
                    act.wait_ge(f_max, head * NT + t + 1)
                    act.activation(F[:, t, :], bank[SF[t]][:, 0:N], ACT.Exp, bias=neg_mx[:, t:t + 1],
                                   scale=FFN_SCALE, accum_out=row_sum[:, t:t + 1]).then_inc(f_exp, 1)

            def fv_hi_of(head):
                act.wait_ge(v_gated, head * 6 + 6)
                act.activation(v2_hi[:, :, 0:P], v_sum, ACT.Copy).then_inc(fv_hi_done, 1)

            def f_pT_hi_of(head, banks=TF):
                for m in range(NT):
                    act.wait_ge(f_probs_T, head * NT + m + 1)
                    act.activation(pT_hi[:, m, :], bank[banks[m]][:, 0:N], ACT.Copy).then_inc(f_pT_hi, 1)

            def context_of(head):
                act.wait_ge(f_context, head + 1)
                act.activation(context, bank[CF][:, 0:N], ACT.Copy).then_inc(context_ready, 1)

            def gc_hi_of(head, e):
                act.wait_ge(gated_ready, head * FE + e + 1)
                act.activation(gc_hi[:, e, :], gated[:, e % 2, :], ACT.Copy).then_inc(gc_hi_done, 1)

            hi_fixed(U_HEAD + 2)
            hi_fixed(U_HEAD + 3)
            f_hi_of(q2_hi, QF, fq_hi_done, U_HEAD + 1)
            hi_fixed(U_HEAD + 4)
            f_hi_of(k2_hi, KF, fk_hi_done, U_HEAD + 2)

            def load_gate_rows(head):
                act.dma_start(gate_rows,
                              gate_rows_dram[bass.ds(head * FE, FE), :].partition_broadcast(P)).then_inc(rows_ready, 16)

            for i in range(3, 7):
                hi_fixed(U_HEAD + i + 2)
            act.wait_ge(gateT_ready, 1)
            act.dma_start(gate_rows_dram, gateT).then_inc(gates_stored, 16)
            f_exp_of(0)
            hi_fixed(U_HEAD + 9)
            act.wait_ge(gates_stored, 16)
            load_gate_rows(0)
            hi_fixed(U_HEAD + 10)
            hi_fixed(U_HEAD + 11)
            fv_hi_of(0)
            f_pT_hi_of(0, OF[0])
            with act.Fori(1, FH) as h:
                base = (U_LOOP - BODY_UNITS, h)
                hi_at(base, 2, BODY_UNITS)
                context_of(h - 1)
                for e in range(4):
                    gc_hi_of(h - 1, e)
                hi_at(base, 3, BODY_UNITS)
                f_hi_of(q2_hi, QF, fq_hi_done, h * BODY_UNITS + (U_LOOP - BODY_UNITS + 1))
                gc_hi_of(h - 1, 4)
                gc_hi_of(h - 1, 5)
                hi_at(base, 4, BODY_UNITS)
                f_hi_of(k2_hi, KF, fk_hi_done, h * BODY_UNITS + (U_LOOP - BODY_UNITS + 2))
                gc_hi_of(h - 1, 6)
                gc_hi_of(h - 1, 7)
                load_gate_rows(h)
                for i in range(5, 9):
                    hi_at(base, i, BODY_UNITS)
                f_exp_of(h)
                for i in range(9, 14):
                    hi_at(base, i, BODY_UNITS)
                fv_hi_of(h)
                for i in range(14, 17):
                    hi_at(base, i, BODY_UNITS)
                f_pT_hi_of(h)
                for i in range(17, 20):
                    hi_at(base, i, BODY_UNITS)
            hi_fixed(U_LAST + 2)
            context_of(FH - 1)
            for e in range(FE):
                gc_hi_of(FH - 1, e)
                if e in (3, 7):
                    hi_fixed(U_LAST + 3 + e // 4)
            for u in range(U_LAST + 5, UNITS):
                hi_fixed(u)

        @block.vector
        def _(dve):
            step = Tally(dve_step)

            def settled():
                dve.wait_ge(step.sem, step.value())

            dve.wait_ge(consts_landed, 16 * 4)
            dve.scalar_tensor_tensor(etw_abs[:], etw[:], -1.0, etw[:], ALU.mult, ALU.max).then_inc(etw_abs_ready, 1)

            def layer_stats(t, f):
                step.add(dve.bn_stats(stats[:, t, f, :], x[:, t, f * HALF:(f + 1) * HALF]))

            def layer_apply():
                settled()
                for t in range(NT):
                    step.add(dve.bn_aggr(moments[:, t, :], stats[:, t].rearrange("p f s -> p (f s)")))
                settled()
                dve.tensor_scalar(var_eps[:], moments[:, :, 1], EPS, None, ALU.add).then_inc(var_ready, 1)

            def layer_write(turn):
                dve.wait_ge(rstd_ready, turn + 1)
                for t in range(NT):
                    dve.tensor_scalar(normed[:, t, :], x[:, t, :], moments[:, t, 0:1], rstd[:, t:t + 1],
                                      ALU.subtract, ALU.mult).then_inc(normed_ready, 1)

            def hT_los(base):
                for k in range(KT):
                    dve.wait_ge(hT_hi_done, base + k + 1)
                    dve.tensor_tensor(hT_lo[:, k, :], bank[LN_BANKS[k % 4]][:, 0:N], hT_hi[:, k, :].bitcast(fp32),
                                      ALU.subtract).then_inc(hT_lo_done, 1)

            for t in range(NT):
                dve.wait_ge(x_landed[t], 16)
                for f in range(2):
                    layer_stats(t, f)
            layer_apply()
            dve.wait_ge(etw_exp, 1)
            dve.tensor_scalar(w8[:], w8[:], 1.0, None, ALU.add).then_inc(etw_exp1, 1)
            layer_write(0)
            hT_los(0)
            dve.wait_ge(etw_log, 1)
            step.add(dve.scalar_tensor_tensor(w8[:], etw[:], 0.0, etw_abs[:], ALU.max, ALU.add))
            settled()
            step.add(dve.tensor_scalar(w8[:], w8[:], 8.0, None, ALU.mult))
            dve.wait_ge(bo_landed, 16)
            dve.wait_ge(normed_ready, NT)
            for t in range(NT):
                last = dve.tensor_tensor(x[:, t, :], x[:, t, :], bo_row, ALU.add)
                if t < NT - 1:
                    step.add(last)
            last.then_inc(bo_added, 1)
            dve.wait_ge(pool_consts, 15)
            step.add(dve.tensor_copy(iota[:], iota_i[:]))
            step.add(dve.tensor_copy(table[:, :, 1], edge[:, 0, :]))
            step.add(dve.tensor_copy(table[:, :, 2], edge[:, 1, :]))
            step.add(dve.tensor_scalar(code[:], edge[:, 2, :], 3.0, None, ALU.add))
            settled()
            step.add(dve.scalar_tensor_tensor(table[:, :, 0], table[:, :, 1], float(N), table[:, :, 2], ALU.mult,
                                              ALU.add))
            step.add(dve.tensor_scalar(code[:], code[:], 3, None, ALU.bitwise_and))
            settled()
            step.add(dve.tensor_tensor(code[:], code[:], chunk_base[:], ALU.add))
            settled()
            step.add(dve.tensor_scalar(code[:], code[:], 23, None, ALU.logical_shift_left))
            settled()
            step.add(dve.tensor_copy(table[:, :, 3], code[:].bitcast(fp32)))
            step.add(dve.memset(v2_hi[:].bitcast(fp32), 0.0))
            dve.memset(v2_lo[:].bitcast(fp32), 0.0).then_inc(v2_cleared, 1)

            def qkv_lo_of(j, i, dst, hi):
                dve.wait_ge(qkv_hi_done, j * 3 + i + 1)
                dve.scalar_tensor_tensor(dst[:, j, :], bank[i][:, 0:N], bias[:, i, bass.ds(j, 1)],
                                         hi[:, j, :].bitcast(fp32), ALU.add, ALU.subtract).then_inc(qkv_lo_done, 1)

            settled()
            with dve.Fori(0, PAIRS) as j:
                step.enter(j, 5)
                dve.wait_ge(rows_landed, j * 32 + 32)
                dve.scalar_tensor_tensor(keys.rearrange("p c q -> p (c q)"), rows[:, 0, :], float(N), rows[:, 1, :],
                                         ALU.mult, ALU.add).then_inc(keys_made, 1)
                step.add(dve.tensor_copy(now[:], table[:, bass.ds(j * PIECE, PIECE), :]))
                settled()
                dve.wait_ge(keys_made, j + 1)
                step.add(dve.tensor_tensor(keys, keys, now[:, :, 0:1].to_broadcast([P, PIECE, P]), ALU.is_equal))
                settled()
                step.add(dve.tensor_tensor(keys, keys, later[:].unsqueeze(1).to_broadcast([P, PIECE, P]), ALU.mult))
                settled()
                step.add(dve.tensor_reduce(dup[:], keys, AX, ALU.max))
                settled()
                step.add(dve.scalar_tensor_tensor(weight[:], dup[:], 0.0, now[:, :, 3], ALU.is_equal, ALU.mult))
                settled()
                qkv_lo_of(j, 0, qT_lo, qT_hi)
                dve.wait_ge(hot_used, j + 1)
                for c in range(PIECE):
                    dve.tensor_scalar(hot[:, 0, c, :], iota[:], now[:, c, 1:2], weight[:, c:c + 1], ALU.is_equal,
                                      ALU.mult).then_inc(hot_ready, 1)
                    dve.tensor_scalar(hot[:, 1, c, :], iota[:], now[:, c, 2:3], None,
                                      ALU.is_equal).then_inc(hot_ready, 1)
                qkv_lo_of(j, 1, kT_lo, kT_hi)
                qkv_lo_of(j, 2, vT_lo, vT_hi)
                dve.wait_ge(hot_ready, j * (2 * PIECE) + 2 * PIECE)
            step.leave(PAIRS)

            def split_lo(dst, src, hi, b, done):
                if b is None:
                    dve.tensor_tensor(dst, src, hi.bitcast(fp32), ALU.subtract).then_inc(done, 1)
                else:
                    dve.scalar_tensor_tensor(dst, src, b, hi.bitcast(fp32), ALU.add, ALU.subtract).then_inc(done, 1)

            def v2_lo_of(pair):
                dve.wait_ge(v2_hi_done, pair + 1)
                split_lo(v2_lo.rearrange("p t (a d) -> p t a d", a=2)[:, :, :, 0:GD],
                         bank[7][:, 0:N].rearrange("p (t a d) -> p t a d", t=NT, a=2),
                         v2_hi.rearrange("p t (a d) -> p t a d", a=2)[:, :, :, 0:GD], None, v2_lo_done)

            def pT_lo_of(pair, head):
                for m in range(NT):
                    dve.wait_ge(pT_hi_done, pair * 6 + NT * head + m + 1)
                    split_lo(pT_lo[:, m, :], bank[NT * head + m][:, 0:N], pT_hi[:, m, :], None, pT_lo_done)

            def max_of(pair, head):
                for t in range(NT):
                    c = NT * head + t
                    dve.wait_ge(scores_done, pair * 6 + c + 1)
                    step.add(dve.memset(holds[:, c:c + 1], 0.0))
                    dve.wait_ge(mask_ready, 1)
                    step.add(dve.tensor_tensor_reduce(S[:, c, :], bank[c][:, 0:N], mask8[:, t, :], scale=GNN_SCALE,
                                                      scalar=-3e38, op0=ALU.add, op1=ALU.max,
                                                      accum_out=mx[:, c:c + 1]))
                settled()
                dve.tensor_scalar(neg_mx[:, NT * head:NT * head + NT], mx[:, NT * head:NT * head + NT], -1.0, None,
                                  ALU.mult).then_inc(max_ready, 1)

            def norm_of(pair, head):
                cs = slice(NT * head, NT * head + NT)
                dve.wait_ge(exp_done, pair * 6 + NT * head + NT)
                step.add(dve.reciprocal(inv_sum[:, cs], row_sum[:, cs]))
                settled()
                for c in range(NT * head, NT * head + NT):
                    dve.tensor_scalar(S[:, c, :], S[:, c, :], inv_sum[:, c:c + 1], None,
                                      ALU.mult).then_inc(norm_done, 1)

            def v2T_of(pair, b):
                dve.wait_ge(unit_used, pair * 3 + (U_PAIR + 3))
                dve.tensor_scalar(v2T[:], bank[7][:, 0:N], b, None, ALU.add).then_inc(v2T_ready, 1)

            def q2_lo_of(pair, b):
                dve.wait_ge(q2_hi_done, pair + 1)
                split_lo(q2_lo[:], bank[6][:, 0:N], q2_hi[:], b, q2_lo_done)

            def k2_lo_of(pair, b):
                dve.wait_ge(k2_hi_done, pair + 1)
                split_lo(k2_lo[:], bank[6][:, 0:N], k2_hi[:], b, k2_lo_done)

            def oT_lo_of(pair, at):
                dve.wait_ge(oT_hi_done, pair + 1)
                split_lo(oT_lo[:, at, :], bank[7][:, 0:N], oT_hi[:, at, :], None, oT_lo_done)

            q2_lo_of(0, bias[:, 3, 0:1])
            dve.wait_ge(rows_landed, 32 * (PAIRS + 1))
            dve.wait_ge(counts_done, 1)
            for t in range(NT):
                step.add(dve.tensor_copy(counts[:, t, :], bank[3 + t][:, 0:N]))
            settled()
            flat = counts.rearrange("p t n -> p (t n)")
            mask_flat = mask8[:].rearrange("p t n -> p (t n)")
            step.add(dve.tensor_scalar(types, flat.bitcast(int32), 23, 3, ALU.logical_shift_right, ALU.bitwise_and))
            step.add(dve.tensor_scalar(mask_flat, flat, 0.0, NO_EDGE, ALU.is_equal, ALU.mult))
            settled()
            k2_lo_of(0, bias[:, 4, 0:1])
            for k in range(4):
                step.add(dve.tensor_scalar(picked, types, float(k), w8[:, k:k + 1], ALU.is_equal, ALU.mult))
                settled()
                last = dve.tensor_tensor(mask_flat, mask_flat, picked, ALU.add)
                if k < 3:
                    step.add(last)
                    settled()
            last.then_inc(mask_ready, 1)
            max_of(0, 0)
            max_of(0, 1)
            norm_of(0, 0)
            norm_of(0, 1)
            v2T_of(0, bias[:, 5, 0:1])
            with dve.Fori(1, PAIRS) as j:
                step.enter(j - 1, 14)
                q2_lo_of(j, bias[:, 3, bass.ds(j, 1)])
                v2_lo_of(j - 1)
                pT_lo_of(j - 1, 0)
                k2_lo_of(j, bias[:, 4, bass.ds(j, 1)])
                pT_lo_of(j - 1, 1)
                max_of(j, 0)
                oT_lo_of(j - 1, j - 1)
                max_of(j, 1)
                norm_of(j, 0)
                norm_of(j, 1)
                v2T_of(j, bias[:, 5, bass.ds(j, 1)])
            step.leave(PAIRS - 1)
            v2_lo_of(PAIRS - 1)
            pT_lo_of(PAIRS - 1, 0)
            pT_lo_of(PAIRS - 1, 1)
            oT_lo_of(PAIRS - 1, PAIRS - 1)

            for f in range(2):
                dve.wait_ge(unit_used, U_WO + 4 * f + 4)
                for t in range(NT):
                    dve.tensor_tensor(x[:, t, f * HALF:(f + 1) * HALF], bank[3 * f + t][:, 0:HALF],
                                      x[:, t, f * HALF:(f + 1) * HALF], ALU.add).then_inc(out_added, 1)
                dve.wait_ge(out_added, NT * f + NT)
                for t in range(NT):
                    layer_stats(t, f)
            layer_apply()
            layer_write(1)
            hT_los(KT)

            G = NT * GROUPS
            probs, ranked, pick1, rest, pick2 = (route[:, a] for a in range(5))
            top1, top2, rank, total, scale1, scale2 = (best[:, a, :] for a in range(6))

            def spread(a):
                return a.unsqueeze(2).to_broadcast([P, G, FE])

            dve.wait_ge(router_exp, 1)
            step.add(dve.tensor_scalar(ranked, probs, 1.0, None, ALU.add))
            settled()
            step.add(dve.reciprocal(probs, ranked))
            settled()
            for left, top, pick in ((probs, top1, pick1), (rest, top2, pick2)):
                step.add(dve.tensor_reduce(top, left, AX, ALU.max))
                settled()
                step.add(dve.tensor_tensor(ranked, left, spread(top), ALU.is_equal))
                settled()
                step.add(dve.tensor_tensor(ranked, ranked, desc[:].unsqueeze(1).to_broadcast([P, G, FE]), ALU.mult))
                settled()
                step.add(dve.tensor_reduce(rank, ranked, AX, ALU.max))
                settled()
                step.add(dve.tensor_tensor(pick, ranked, spread(rank), ALU.is_equal))
                settled()
                if pick is pick1:
                    step.add(dve.scalar_tensor_tensor(rest.rearrange("p g e -> p (g e)"),
                                                      pick1.rearrange("p g e -> p (g e)"), -2.0,
                                                      probs.rearrange("p g e -> p (g e)"), ALU.mult, ALU.add))
                    settled()
            step.add(dve.tensor_tensor(total, top1, top2, ALU.add))
            settled()
            step.add(dve.tensor_scalar(total, total, 1e-9, None, ALU.max))
            settled()
            step.add(dve.reciprocal(rank, total))
            settled()
            step.add(dve.tensor_tensor(scale1, top1, rank, ALU.mult))
            step.add(dve.tensor_tensor(scale2, top2, rank, ALU.mult))
            settled()
            step.add(dve.tensor_scalar(best[:, 4:6, :], best[:, 4:6, :], rs[:, 0:1], None, ALU.mult))
            settled()
            step.add(dve.tensor_tensor(pick1, pick1, spread(scale1), ALU.mult))
            step.add(dve.tensor_tensor(pick2, pick2, spread(scale2), ALU.mult))
            settled()
            dve.tensor_tensor(gates[:].rearrange("p t (g e) -> p (t g) e", e=FE), pick1, pick2,
                              ALU.add).then_inc(gates_ready, 1)

            def f_lo_of(dst, hi, b, hi_done, lo_done, head):
                dve.wait_ge(hi_done, head + 1)
                split_lo(dst[:], bank[b][:, 0:N], hi[:], None, lo_done)

            def gate_copy(head):
                step.add(dve.tensor_copy(v_gate[:], gates[:, :, bass.ds(head * FE, FE)]))

            def gate_values(head, g, need):
                dve.wait_ge(unit_used, need)
                for e in range(4):
                    settled()
                    for t in range(NT):
                        src = bank[VF[g][t]][:, e * P:(e + 1) * P]
                        col = v_gate[:, t, 4 * g + e:4 * g + e + 1]
                        if g == 0 and e == 0:
                            ins = dve.tensor_scalar(v_sum[:, t, :], src, col, None, ALU.mult)
                        else:
                            ins = dve.scalar_tensor_tensor(v_sum[:, t, :], src, col, v_sum[:, t, :], ALU.mult,
                                                           ALU.add)
                        if e < 3:
                            step.add(ins)
                        else:
                            ins.then_inc(v_gated, 1)
                dve.wait_ge(v_gated, head * 6 + 3 * g + 3)

            def f_max_of(head):
                for t in range(NT):
                    dve.wait_ge(f_scores, head * NT + t + 1)
                    step.add(dve.tensor_reduce(mx[:, t:t + 1], bank[SF[t]][:, 0:N], AX, ALU.max))
                    settled()
                    dve.tensor_scalar(neg_mx[:, t:t + 1], mx[:, t:t + 1], -FFN_SCALE, None,
                                      ALU.mult).then_inc(f_max, 1)

            def f_norm_of(head):
                dve.wait_ge(f_exp, head * NT + NT)
                step.add(dve.reciprocal(inv_sum[:, 0:NT], row_sum[:, 0:NT]))
                settled()
                for t in range(NT):
                    dve.tensor_scalar(F[:, t, :], F[:, t, :], inv_sum[:, t:t + 1], None,
                                      ALU.mult).then_inc(f_norm, 1)

            def fv_lo_of(head):
                dve.wait_ge(fv_hi_done, head + 1)
                split_lo(v2_lo[:, :, 0:P], v_sum, v2_hi[:, :, 0:P], None, fv_lo_done)

            def f_pT_lo_of(head, banks=TF):
                for m in range(NT):
                    dve.wait_ge(f_pT_hi, head * NT + m + 1)
                    split_lo(pT_lo[:, m, :], bank[banks[m]][:, 0:N], pT_hi[:, m, :], None, f_pT_lo)

            def gate_context(head, e):
                if e == 0:
                    dve.wait_ge(context_ready, head + 1)
                    dve.wait_ge(rows_ready, head * 16 + 16)
                if e >= 2:
                    dve.wait_ge(gc_lo_done, head * FE + e - 1)
                dve.tensor_tensor(gated[:, e % 2, :], context, gate_rows[:, e, :], ALU.mult).then_inc(gated_ready, 1)

            def gc_lo_of(head, e):
                dve.wait_ge(gc_hi_done, head * FE + e + 1)
                split_lo(gc_lo[:, e, :], gated[:, e % 2, :], gc_hi[:, e, :], None, gc_lo_done)

            def gate_contexts(head):
                gate_context(head, 0)
                for e in range(FE):
                    if e + 1 < FE:
                        gate_context(head, e + 1)
                    gc_lo_of(head, e)

            def add_out(head, f, need):
                dve.wait_ge(unit_used, need)
                for t in range(NT):
                    dve.tensor_tensor(x[:, t, f * HALF:(f + 1) * HALF], bank[OF[f][t]][:, 0:HALF],
                                      x[:, t, f * HALF:(f + 1) * HALF], ALU.add).then_inc(out_added, 1)

            dve.wait_ge(gates_ready, 1)
            gate_copy(0)
            f_lo_of(q2_lo, q2_hi, QF, fq_hi_done, fq_lo_done, 0)
            f_lo_of(k2_lo, k2_hi, KF, fk_hi_done, fk_lo_done, 0)
            dve.wait_ge(gates_T, 1)
            dve.tensor_copy(gateT, bank[QF][0:FH * FE, 0:N]).then_inc(gateT_ready, 1)
            gate_values(0, 0, U_HEAD + 6)
            f_max_of(0)
            f_norm_of(0)
            gate_values(0, 1, U_HEAD + 10)
            fv_lo_of(0)
            f_pT_lo_of(0, OF[0])
            with dve.Fori(1, FH) as h:
                step.enter(h - 1, 1 + 18 + 3 + 1)
                gate_copy(h)
                gate_contexts(h - 1)
                f_lo_of(q2_lo, q2_hi, QF, fq_hi_done, fq_lo_done, h)
                f_lo_of(k2_lo, k2_hi, KF, fk_hi_done, fk_lo_done, h)
                gate_values(h, 0, h * BODY_UNITS + (U_LOOP - BODY_UNITS + 6))
                f_max_of(h)
                f_norm_of(h)
                gate_values(h, 1, h * BODY_UNITS + (U_LOOP - BODY_UNITS + 10))
                fv_lo_of(h)
                dve.wait_ge(out_added, h * 6)
                add_out(h - 1, 0, h * BODY_UNITS + (U_LOOP - BODY_UNITS + 14))
                f_pT_lo_of(h)
                add_out(h - 1, 1, h * BODY_UNITS + (U_LOOP - BODY_UNITS + 18))
            step.leave(FH - 1)
            gate_contexts(FH - 1)
            dve.wait_ge(out_added, FH * 6)
            add_out(FH - 1, 0, U_LAST + 4)
            add_out(FH - 1, 1, U_LAST + 8)

        @block.tensor
        def _(pe):
            def three(dst, a_hi, a_lo, b_hi, b_lo, first, last):
                pe.matmul(dst, a_hi, b_hi, start=first, stop=False)
                pe.matmul(dst, a_hi, b_lo, start=False, stop=False)
                return pe.matmul(dst, a_lo, b_hi, start=False, stop=last)

            def column_unit(u, s, dst, b_hi, b_lo):
                pe.wait_ge(lo_ready, u + 1)
                for k in range(KT):
                    c = slice(k * P, (k + 1) * P)
                    last = three(dst[:, 0:N], w_hi[:, s, c], w_lo[:, s, c], b_hi[:, k, :], b_lo[:, k, :], k == 0,
                                 k == KT - 1)
                last.then_inc(unit_used, 1)

            def row_unit(u, s, banks, a_hi, a_lo, i, third=None):
                pe.wait_ge(lo_ready, u + 1)
                for kk in range(2):
                    c = slice(kk * HALF, (kk + 1) * HALF)
                    for t in range(NT):
                        tok = slice(t * P, (t + 1) * P)
                        k = 2 * i + kk
                        if third and t == 2 and k == 0:
                            pe.wait_ge(*third)
                        last = three(bank[banks[t]][:, 0:HALF], a_hi[:, k, tok], a_lo[:, k, tok], w_hi[:, s, c],
                                     w_lo[:, s, c], k == 0, k == KT - 1)
                last.then_inc(unit_used, 1)

            def turn(dst, src):
                return pe.transpose(dst, src, ident[:])

            def normed_turns(base):
                pe.wait_ge(normed_ready, NT * (base // KT) + NT)
                for k in range(KT):
                    if k >= 4:
                        pe.wait_ge(hT_lo_done, base + k - 3)
                    for t in range(NT):
                        last = turn(bank[LN_BANKS[k % 4]][:, t * P:(t + 1) * P], normed[:, t, k * P:(k + 1) * P])
                    last.then_inc(normed_T, 1)

            pe.wait_ge(pool_consts, 15)
            normed_turns(0)
            def self_edges(first):
                for t in range(NT):
                    last = pe.matmul(bank[3 + t][:, 0:N], eye_self[:],
                                     eye_wide[:, (2 - t) * P:(5 - t) * P], start=first, stop=not first)
                return last

            self_edges(True).then_inc(hot_used, 1)
            pe.wait_ge(hT_lo_done, KT)
            with pe.Fori(0, PAIRS) as j:
                for i in range(3):
                    column_unit(j * 3 + i, i, bank[i], hT_hi, hT_lo)
                for c in range(PIECE):
                    pe.wait_ge(hot_ready, j * (2 * PIECE) + 2 * c + 2)
                    for t in range(NT):
                        last = pe.matmul(bank[3 + t][:, 0:N], hot[:, 0, c, t * P:(t + 1) * P], hot[:, 1, c, :],
                                         start=False, stop=False)
                last.then_inc(hot_used, 1)
                pe.wait_ge(qkv_lo_done, j * 3 + 3)
            self_edges(False).then_inc(counts_done, 1)

            def scores_of(pair, head):
                p = slice(GD * head, GD * head + GD)
                if head == 0:
                    pe.wait_ge(q2_lo_done, pair + 1)
                    pe.wait_ge(k2_lo_done, pair + 1)
                for t in range(NT):
                    tok = slice(t * P, (t + 1) * P)
                    three(bank[NT * head + t][:, 0:N], q2_hi[p, tok], q2_lo[p, tok], k2_hi[p, :], k2_lo[p, :], True,
                          True).then_inc(scores_done, 1)

            def probs_of(pair, head):
                pe.wait_ge(norm_done, pair * 6 + NT * head + NT)
                for m in range(NT):
                    for t in range(NT):
                        last = turn(bank[NT * head + m][:, t * P:(t + 1) * P],
                                    S[:, NT * head + t, m * P:(m + 1) * P])
                    last.then_inc(probs_T, 1)

            def values_back(pair):
                pe.wait_ge(v2T_ready, pair + 1)
                for t in range(NT):
                    last = turn(bank[7][:, t * P:(t + 1) * P], v2T[:, t * P:(t + 1) * P])
                last.then_inc(v2_back, 1)

            def attend(pair, head):
                if head == 0:
                    pe.wait_ge(v2_lo_done, pair + 1)
                c = slice(GD * head, GD * head + P)
                for m in range(NT):
                    pe.wait_ge(pT_lo_done, pair * 6 + NT * head + m + 1)
                    last = three(bank[7][:, 0:N], v2_hi[:, m, c], v2_lo[:, m, c], pT_hi[:, m, :], pT_lo[:, m, :],
                                 head == 0 and m == 0, head == 1 and m == NT - 1)
                last.then_inc(pair_out if head else pair_out_first, 1)

            pe.wait_ge(v2_cleared, 1)
            column_unit(U_PAIR, 0, bank[6], qT_hi, qT_lo)
            pe.wait_ge(q2_lo_done, 1)
            column_unit(U_PAIR + 1, 1, bank[6], kT_hi, kT_lo)
            scores_of(0, 0)
            scores_of(0, 1)
            column_unit(U_PAIR + 2, 2, bank[7], vT_hi, vT_lo)
            with pe.Fori(1, PAIRS) as j:
                pe.wait_ge(k2_lo_done, j)
                column_unit(j * 3 + U_PAIR, 0, bank[6], qT_hi, qT_lo)
                values_back(j - 1)
                probs_of(j - 1, 0)
                pe.wait_ge(q2_lo_done, j + 1)
                column_unit(j * 3 + (U_PAIR + 1), 1, bank[6], kT_hi, kT_lo)
                attend(j - 1, 0)
                probs_of(j - 1, 1)
                scores_of(j, 0)
                attend(j - 1, 1)
                scores_of(j, 1)
                pe.wait_ge(oT_lo_done, j)
                column_unit(j * 3 + (U_PAIR + 2), 2, bank[7], vT_hi, vT_lo)
            values_back(PAIRS - 1)
            probs_of(PAIRS - 1, 0)
            attend(PAIRS - 1, 0)
            probs_of(PAIRS - 1, 1)
            attend(PAIRS - 1, 1)
            pe.wait_ge(oT_lo_done, PAIRS)
            for f in range(2):
                for i in range(4):
                    u = U_WO + 4 * f + i
                    row_unit(u, u % RING, (3 * f, 3 * f + 1, 3 * f + 2), oT_hi, oT_lo, i)
            normed_turns(KT)
            pe.wait_ge(hT_lo_done, 2 * KT)
            pe.wait_ge(lo_ready, U_ROUTER + 1)
            for t in range(NT):
                tok = slice(t * P, (t + 1) * P)
                for k in range(KT):
                    c = slice(k * P, (k + 1) * P)
                    s = U_ROUTER % RING
                    last = three(bank[RF][:, tok], hT_hi[:, k, tok], hT_lo[:, k, tok], w_hi[:, s, c], w_lo[:, s, c],
                                 k == 0, k == KT - 1)
            last.then_inc(unit_used, 1)

            def values_units(head, g, u, s):
                for i in range(4):
                    row_unit(u + 4 * g + i, (s + 4 * g + i) % RING, VF[g], hT_hi, hT_lo, i,
                             (v_gated, head * 6 + 1) if g else None)

            def f_scores_of(head):
                pe.wait_ge(fq_lo_done, head + 1)
                pe.wait_ge(fk_lo_done, head + 1)
                for t in range(NT):
                    tok = slice(t * P, (t + 1) * P)
                    three(bank[SF[t]][:, 0:N], q2_hi[:, tok], q2_lo[:, tok], k2_hi[:], k2_lo[:], True,
                          True).then_inc(f_scores, 1)

            def f_probs_of(head, banks=TF):
                pe.wait_ge(f_norm, head * NT + NT)
                for m in range(NT):
                    for t in range(NT):
                        last = turn(bank[banks[m]][:, t * P:(t + 1) * P], F[:, t, m * P:(m + 1) * P])
                    last.then_inc(f_probs_T, 1)

            def f_attend(head):
                pe.wait_ge(fv_lo_done, head + 1)
                for m in range(NT):
                    pe.wait_ge(f_pT_lo, head * NT + m + 1)
                    last = three(bank[CF][:, 0:N], v2_hi[:, m, 0:P],
                                 v2_lo[:, m, 0:P], pT_hi[:, m, :], pT_lo[:, m, :], m == 0, m == NT - 1)
                last.then_inc(f_context, 1)

            def output_units(head, f, u, s):
                for i in range(4):
                    pe.wait_ge(gc_lo_done, head * FE + 2 * i + 2)
                    row_unit(u + i, (s + i) % RING, OF[f], gc_hi, gc_lo, i,
                             (out_added, head * 6 + 7) if f else None)

            column_unit(U_HEAD, U_HEAD % RING, bank[QF], hT_hi, hT_lo)
            column_unit(U_HEAD + 1, (U_HEAD + 1) % RING, bank[KF], hT_hi, hT_lo)
            values_units(0, 0, U_HEAD + 2, (U_HEAD + 2) % RING)
            f_scores_of(0)
            pe.wait_ge(gates_ready, 1)
            for t in range(NT):
                last = turn(bank[QF][0:FH * FE, t * P:(t + 1) * P], gates[:, t, FH * FE:2 * FH * FE])
            last.then_inc(gates_T, 1)
            pe.wait_ge(gateT_ready, 1)
            values_units(0, 1, U_HEAD + 2, (U_HEAD + 2) % RING)
            pe.wait_ge(v_gated, NT)
            f_probs_of(0, OF[0])
            pe.wait_ge(f_pT_lo, NT)
            f_attend(0)
            with pe.Fori(1, FH) as h:
                u = h * BODY_UNITS + (U_LOOP - BODY_UNITS)
                s = U_LOOP % RING
                column_unit(u, s, bank[QF], hT_hi, hT_lo)
                column_unit(u + 1, (s + 1) % RING, bank[KF], hT_hi, hT_lo)
                pe.wait_ge(context_ready, h)
                pe.wait_ge(out_added, h * 6)
                values_units(h, 0, u + 2, (s + 2) % RING)
                f_scores_of(h)
                values_units(h, 1, u + 2, (s + 2) % RING)
                pe.wait_ge(v_gated, h * 6 + 3)
                pe.wait_ge(f_exp, h * NT + NT)
                output_units(h - 1, 0, u + 10, (s + 10) % RING)
                pe.wait_ge(v_gated, h * 6 + 6)
                f_probs_of(h)
                output_units(h - 1, 1, u + 14, (s + 14) % RING)
                pe.wait_ge(out_added, h * 6 + 2)
                f_attend(h)
            pe.wait_ge(out_added, FH * 6)
            output_units(FH - 1, 0, U_LAST, U_LAST % RING)
            output_units(FH - 1, 1, U_LAST + 4, (U_LAST + 4) % RING)


def kernel(**inputs):
    import numpy as np
    import concourse.bacc as bacc
    from concourse.bass_utils import run_bass_kernel_spmd

    a = {name: np.asarray(value) for name, value in inputs.items()}
    g = {name[len("L0_gnn_"):]: v for name, v in a.items() if name.startswith("L0_gnn_")}
    f = {name[len("L0_ffn_"):]: v for name, v in a.items() if name.startswith("L0_ffn_")}

    def column_units(w):
        o = w.shape[0] // P
        return w.reshape(o, P, KT, P).transpose(0, 3, 2, 1).reshape(o, P, D)

    def row_units(w):
        o = w.shape[1] // HALF
        return w.reshape(4, 2, P, o, HALF).transpose(3, 0, 2, 1, 4).reshape(o * 4, P, D)

    def by_turns(*lots):
        return np.stack(lots, axis=1).reshape(-1, P, D)

    q, k = column_units(f["q_w"]), column_units(f["k_w"])
    v_w = f["v_w"].reshape(FH, FE, D, P).transpose(0, 2, 1, 3).reshape(FH, D, FE * P)
    o_w = f["o_w"].reshape(FH, FE * P, D)
    lots = [by_turns(*(column_units(g[n]) for n in ("wq", "wk", "wv"))),
            by_turns(*(column_units(g[n]) for n in ("wiq", "wik", "wiv"))),
            row_units(g["wo"].T),
            column_units(np.concatenate([f["sel_v_w"], f["sel_o_w"]]))]
    for h in range(FH):
        lots += [q[h:h + 1], k[h:h + 1], row_units(v_w[h])]
        if h:
            lots.append(row_units(o_w[h - 1]))
    lots.append(row_units(o_w[FH - 1]))
    arrays = {
        "x": a["x"],
        "units": np.concatenate(lots),
        "biases": np.stack([g[n].reshape(KT, P).T for n in ("bq", "bk", "bv", "biq", "bik", "biv")], axis=1),
        "bo": g["bo"],
        "edge_type_weights": g["edge_type_weights"],
        "route_scale": f["route_scale"],
        "edge_cols": np.stack([a[n].reshape(CHUNKS, P).T for n in ("src", "dst", "edge_type_5")], axis=1),
        "src_row": np.concatenate([a["src"], a["src"][:PIECE * P]]).reshape(PAIRS + 1, PIECE * P),
        "dst_row": np.concatenate([a["dst"], a["dst"][:PIECE * P]]).reshape(PAIRS + 1, PIECE * P),
    }
    assert arrays["units"].shape == (UNITS, P, D)
    arrays = {name: np.ascontiguousarray(v) for name, v in arrays.items()}
    nc = bacc.Bacc("TRN2", target_bir_lowering=False, num_devices=1)
    args = [nc.dram_tensor(f"in_{name}", v.shape, mybir.dt.from_np(v.dtype), kind="ExternalInput").ap()
            for name, v in arrays.items()]
    out = nc.dram_tensor("out_x", (N, D), mybir.dt.float32, kind="ExternalOutput").ap()
    gnn_switch_kernel(nc, *args, out)
    result = run_bass_kernel_spmd(nc, [{f"in_{name}": v for name, v in arrays.items()}], core_ids=[0])
    return result.results[0]["out_x"]
```

```python
import concourse.bass as bass
from concourse import mybir
from contextlib import ExitStack


P = 128
N = 384
NT = N // P
D = 1024
KT = D // P
HALF = D // 2
EDGES = 6144
CHUNKS = EDGES // P
GD = 64
PAIRS = D // P
FH = 8
FE = 8
GROUPS = 2 * FH
EPS = 1e-5
GNN_SCALE = 1.0 / 8.0
FFN_SCALE = float(P) ** -0.5
NO_EDGE = -(2.0 ** 120)

RING = 3
U_PAIR = 3 * PAIRS
U_WO = U_PAIR + 3 * PAIRS
U_ROUTER = U_WO + 8
U_HEAD = U_ROUTER + 1
HEAD_UNITS = 12
BODY_UNITS = 18
U_LOOP = U_HEAD + HEAD_UNITS
U_LAST = U_LOOP + (FH - 1) * BODY_UNITS - 2
UNITS = U_LAST + 8
assert UNITS % RING == 0 and U_ROUTER % RING == 2 and BODY_UNITS % RING == 0

LN_BANKS = (6, 7, 3, 4, 5, 0)
WO_BANKS = ((3, 4, 5), (0, 1, 2))
LN_STEPS = 2 * NT
RF = 2
GF = 7
QF, KF = 5, 0
VF = ((2, 3, 4), (0, 1, 2))
SF = (5, 6, 7)
TF = (0, 1, 2)
TF_FIRST = (3, 4, 6)
OF = ((3, 4, 5), (6, 7, 3))
OF_LAST = ((0, 1, 2), (5, 6, 7))
CF = 4
PIECE = CHUNKS // PAIRS


class Tally:

    def __init__(self, sem):
        self.sem, self.n, self.turns = sem, 0, 0

    def add(self, instruction):
        instruction.then_inc(self.sem, 1)
        self.n += 1

    def value(self):
        return self.turns + self.n

    def enter(self, turn, per_turn):
        self.start, self.per_turn = self.n, per_turn
        self.turns = turn * per_turn

    def leave(self, turns):
        assert self.n - self.start == self.per_turn, (self.n - self.start, self.per_turn)
        self.n, self.turns = self.start + self.per_turn * turns, 0


def gnn_switch_kernel(nc, x_in, units, biases, bo, edge_type_weights, route_scale, edge_cols, src_row, dst_row, out):
    fp32, f32r, bf16 = mybir.dt.float32, mybir.dt.float32r, mybir.dt.bfloat16
    fp16, int32 = mybir.dt.float16, mybir.dt.int32
    ALU, ACT, AX = mybir.AluOpType, mybir.ActivationFunctionType, mybir.AxisListType.X

    ctx = ExitStack()
    with ctx:
        def sb(name, shape, dt):
            return ctx.enter_context(nc.sbuf_tensor(name, shape, dt))

        def sem(name):
            return ctx.enter_context(nc.semaphore(name))

        w_raw = sb("w_raw", [P, RING, D], fp32)
        w_hi = sb("w_hi", [P, RING, D], f32r)
        w_lo = sb("w_lo", [P, RING, D], f32r)
        hT_hi, hT_lo = sb("hT_hi", [P, KT, N], f32r), sb("hT_lo", [P, KT, N], f32r)
        qT_hi, qT_lo = sb("qT_hi", [P, KT, N], f32r), sb("qT_lo", [P, KT, N], f32r)
        kT_hi, kT_lo = sb("kT_hi", [P, KT, N], f32r), sb("kT_lo", [P, KT, N], f32r)
        vT_hi, vT_lo = sb("vT_hi", [P, KT, N], f32r), sb("vT_lo", [P, KT, N], f32r)
        oT_hi, oT_lo = hT_hi, hT_lo
        gc_hi, gc_lo = qT_hi, qT_lo
        q2_hi, q2_lo = sb("q2_hi", [P, N], f32r), sb("q2_lo", [P, N], f32r)
        k2_hi, k2_lo = sb("k2_hi", [P, N], f32r), sb("k2_lo", [P, N], f32r)
        v2_hi, v2_lo = sb("v2_hi", [P, NT, 2 * P], f32r), sb("v2_lo", [P, NT, 2 * P], f32r)
        pT_hi, pT_lo = sb("pT_hi", [P, 2, NT, N], f32r), sb("pT_lo", [P, 2, NT, N], f32r)
        x = sb("x", [P, NT, D], fp32)
        mask8 = sb("mask8", [P, NT, N], fp32)
        gates = mask8[:, 0, :].rearrange("p (t g) -> p t g", t=NT)
        scratch = sb("scratch", [P, 6144], fp32)
        normed = scratch[:, 3072:6144].rearrange("p (t d) -> p t d", t=NT)
        rows = scratch[:, 0:2 * PIECE * P].bitcast(int32).rearrange("p (a n) -> p a n", a=2)
        keys = scratch[:, 1536:1536 + PIECE * P].rearrange("p (c q) -> p c q", c=PIECE)
        iota_i = scratch[:, 1536:1536 + N].bitcast(int32)
        eye_wide = scratch[:, 2304:2304 + 5 * P // 2].bitcast(bf16)
        table = scratch[:, 2624:2624 + 4 * CHUNKS].rearrange("p (c k) -> p c k", k=4)
        hot = scratch[:, 3072:3072 + PIECE * N].bitcast(bf16).rearrange("p (a c n) -> p a c n", a=2, c=PIECE)
        counts = scratch[:, 0:NT * N].rearrange("p (t n) -> p t n", t=NT)
        types = scratch[:, 1152:2304].bitcast(int32)
        picked = scratch[:, 2304:3456]
        S = scratch[:, 0:6 * N].rearrange("p (t n) -> p t n", t=6)
        picked_2, picked_3 = scratch[:, 3456:4608], scratch[:, 4608:5760]
        v2T = scratch[:, 5760:5760 + N]
        route = scratch[:, 0:3072].rearrange("p (a g e) -> p a g e", a=8, e=FE)
        gate_rows = scratch[:, 0:3072].rearrange("p (e n) -> p e n", e=FE)
        F = scratch[:, 3072:3072 + NT * N].rearrange("p (t n) -> p t n", t=NT)
        gated = scratch[:, 4224:4224 + 2 * N].rearrange("p (b n) -> p b n", b=2)
        context = scratch[:, 4992:4992 + N]
        v_sum = scratch[:, 5376:5376 + N].rearrange("p (t d) -> p t d", t=NT)
        gateT = scratch[0:FH * FE, 5760:5760 + N]
        iota = sb("iota", [P, N], fp16)
        ident = sb("ident", [P, P], fp32)
        later = sb("later", [P, P], fp32)
        eye_self = sb("eye_self", [P, P], bf16)
        desc = sb("desc", [P, FE], fp32)
        chunk_base = sb("chunk_base", [P, CHUNKS], int32)
        bias = sb("bias", [P, 6, KT], fp32)
        edge = sb("edge", [P, 3, CHUNKS], int32)
        now = sb("now", [P, PIECE, 4], fp32)
        dup = sb("dup", [P, PIECE], fp32)
        weight = sb("weight", [P, PIECE], fp32)
        code = sb("code", [P, CHUNKS], int32)
        etw = sb("etw", [P, 4], fp32)
        etw_abs = sb("etw_abs", [P, 4], fp32)
        w8 = sb("w8", [P, 4], fp32)
        rs = sb("rs", [P, 1], fp32)
        stats = sb("stats", [P, NT, 2, 6], fp32)
        moments = sb("moments", [P, NT, 2], fp32)
        var_eps = sb("var_eps", [P, NT], fp32)
        minus_half = sb("minus_half", [P, 1], fp32)
        warm = sb("warm", [P, 1], fp32)
        neg_mean = sb("neg_mean", [P, NT], fp32)
        shift = sb("shift", [P, NT], fp32)
        rstd = sb("rstd", [P, NT], fp32)
        mx = sb("mx", [P, 6], fp32)
        neg_mx = sb("neg_mx", [P, 6], fp32)
        row_sum = sb("row_sum", [P, 6], fp32)
        inv_sum = sb("inv_sum", [P, 6], fp32)
        holds = sb("holds", [P, 6], fp32)
        best = sb("best", [P, 6, 3 * GROUPS], fp32)
        v_gate = sb("v_gate", [P, NT, FE], fp32)

        bank = [ctx.enter_context(nc.psum_tensor(f"bank{i}", [P, 512], fp32)) for i in range(8)]
        gate_rows_dram = nc.dram_tensor("gate_rows_scratch", (FH * FE, N), fp32).ap()

        raw_landed = [sem(f"raw_landed{s}") for s in range(RING)]
        hi_ready, lo_ready, unit_used = sem("hi_ready"), sem("lo_ready"), sem("unit_used")
        x0_landed = sem("x0_landed")
        x_landed = [sem(f"x_landed{t}") for t in range(NT)]
        consts_landed, bo_landed = sem("consts_landed"), sem("bo_landed")
        pool_consts, pool_step, dve_consts = sem("pool_consts"), sem("pool_step"), sem("dve_consts")
        var_ready, rstd_ready, normed_ready = sem("var_ready"), sem("rstd_ready"), sem("normed_ready")
        normed_T, hT_hi_done, hT_lo_done = sem("normed_T"), sem("hT_hi_done"), sem("hT_lo_done")
        tile_done, act_warm, last_normed = sem("tile_done"), sem("act_warm"), sem("last_normed")
        qkv_hi_done, qkv_lo_done = sem("qkv_hi_done"), sem("qkv_lo_done")
        rows_landed, keys_made = sem("rows_landed"), sem("keys_made")
        hot_ready, hot_used, counts_done = sem("hot_ready"), sem("hot_used"), sem("counts_done")
        etw_abs_ready, etw_exp, etw_exp1, etw_log = (sem("etw_abs_ready"), sem("etw_exp"), sem("etw_exp1"),
                                                     sem("etw_log"))
        picks_ready, picks_added = sem("picks_ready"), sem("picks_added")
        v2_cleared, mask_ready, dve_step = sem("v2_cleared"), sem("mask_ready"), sem("dve_step")
        q2_hi_done, q2_lo_done, k2_hi_done, k2_lo_done = (sem("q2_hi_done"), sem("q2_lo_done"), sem("k2_hi_done"),
                                                          sem("k2_lo_done"))
        v2T_ready, v2_back, v2_hi_done, v2_lo_done = (sem("v2T_ready"), sem("v2_back"), sem("v2_hi_done"),
                                                      sem("v2_lo_done"))
        scores_done, max_ready, exp_done, norm_done = (sem("scores_done"), sem("max_ready"), sem("exp_done"),
                                                       sem("norm_done"))
        probs_T, pT_hi_done, pT_lo_done = sem("probs_T"), sem("pT_hi_done"), sem("pT_lo_done")
        pair_out = sem("pair_out")
        oT_hi_done, oT_lo_done, bo_added = sem("oT_hi_done"), sem("oT_lo_done"), sem("bo_added")
        router_exp, gates_ready, gates_T, gateT_ready = (sem("router_exp"), sem("gates_ready"), sem("gates_T"),
                                                         sem("gateT_ready"))
        gates_stored, rows_ready = sem("gates_stored"), sem("rows_ready")
        fq_hi_done, fq_lo_done, fk_hi_done, fk_lo_done = (sem("fq_hi_done"), sem("fq_lo_done"), sem("fk_hi_done"),
                                                          sem("fk_lo_done"))
        v_gated, fv_hi_done, fv_lo_done = sem("v_gated"), sem("fv_hi_done"), sem("fv_lo_done")
        f_scores, f_max, f_exp, f_norm = sem("f_scores"), sem("f_max"), sem("f_exp"), sem("f_norm")
        f_probs_T, f_pT_hi, f_pT_lo = sem("f_probs_T"), sem("f_pT_hi"), sem("f_pT_lo")
        f_context, context_ready = sem("f_context"), sem("context_ready")
        gated_ready, gc_hi_done, gc_lo_done, out_added = (sem("gated_ready"), sem("gc_hi_done"), sem("gc_lo_done"),
                                                          sem("out_added"))
        out_stored = sem("out_stored")

        bo_row = mask8[:].rearrange("p t n -> p (t n)")[:, 0:D]

        x_tiles = x_in.rearrange("(t p) d -> p t d", p=P)
        out_tiles = out.rearrange("(t p) d -> p t d", p=P)

        block = ctx.enter_context(nc.Block())

        @block.sync
        def _(sp):
            def load_x(t):
                sp.dma_start(x[:, t, :], x_tiles[:, t, :]).then_inc(x_landed[t], 16)

            def load_first(s):
                sp.dma_start(w_raw[:, s, :], units[s]).then_inc(raw_landed[s], 16)

            for f in range(2):
                cols = slice(f * HALF, (f + 1) * HALF)
                sp.dma_start(x[:, 0, cols], x_tiles[:, 0, cols]).then_inc((x0_landed, x_landed[0])[f], 16)
            load_x(1)
            load_x(2)
            load_first(0)
            load_first(1)
            sp.dma_start(rows[:, 0, :], src_row[0].partition_broadcast(P)).then_inc(rows_landed, 16)
            sp.dma_start(rows[:, 1, :], dst_row[0].partition_broadcast(P)).then_inc(rows_landed, 16)
            load_first(2)
            sp.dma_start(bo_row, bo.partition_broadcast(P)).then_inc(bo_landed, 16)
            with sp.Fori(1, UNITS // RING) as turn:
                for s in range(RING):
                    sp.wait_ge(lo_ready, turn * RING + (s - RING + 1))
                    sp.dma_start(w_raw[:, s, :], units[turn * RING + s]).then_inc(raw_landed[s], 16)
            for f in range(2):
                for t in range(NT):
                    sp.wait_ge(out_added, 6 * FH + NT * f + t + 1)
                    sp.dma_start(out_tiles[:, t, f * HALF:(f + 1) * HALF],
                                 x[:, t, f * HALF:(f + 1) * HALF]).then_inc(out_stored, 16)
            sp.wait_ge(out_stored, 16 * 2 * NT)

        @block.gpsimd
        def _(pool):
            pool.memset(minus_half[:], -0.5).then_inc(pool_consts, 1)
            pool.memset(ident[:], 0.0).then_inc(pool_step, 1)
            pool.wait_ge(pool_step, 1)
            pool.affine_select(out=ident[:], in_=ident[:], compare_op=ALU.not_equal, fill=1.0, base=0,
                               pattern=[[-1, P]], channel_multiplier=1).then_inc(pool_consts, 1)

            def rstds_of(turn):
                for t in range(NT):
                    n = turn * NT + t + 1
                    pool.wait_ge(var_ready, n)
                    pool.tensor_tensor(rstd[:, t:t + 1], var_eps[:, t:t + 1], minus_half[:],
                                       ALU.pow).then_inc(pool_step, 1)
                    pool.wait_ge(pool_step, 4 + n)
                    pool.tensor_tensor(shift[:, t:t + 1], neg_mean[:, t:t + 1], rstd[:, t:t + 1],
                                       ALU.mult).then_inc(rstd_ready, 1)

            def make_lo(u, s):
                pool.wait_ge(hi_ready, u + 1)
                pool.tensor_tensor(w_lo[:, s, :], w_raw[:, s, :], w_hi[:, s, :].bitcast(fp32),
                                   ALU.subtract).then_inc(lo_ready, 1)

            pool.memset(later[:], 1.0).then_inc(pool_step, 1)
            pool.wait_ge(pool_step, 2)
            pool.affine_select(out=later[:], in_=later[:], compare_op=ALU.is_gt, fill=0.0, base=0,
                               pattern=[[1, P]], channel_multiplier=-1).then_inc(pool_consts, 1)
            pool.iota(iota_i, pattern=[[1, N]], base=0, channel_multiplier=0).then_inc(pool_consts, 1)
            pool.iota(chunk_base[:], pattern=[[4, CHUNKS]], base=32, channel_multiplier=0).then_inc(pool_consts, 1)
            for e in range(FE):
                pool.memset(desc[:, e:e + 1], float(FE - e)).then_inc(pool_consts, 1)
            pool.memset(eye_wide, 0.0).then_inc(pool_step, 1)
            pool.memset(eye_self[:], 0.0).then_inc(pool_step, 1)
            pool.wait_ge(pool_step, 4)
            pool.affine_select(out=eye_wide, in_=eye_wide, compare_op=ALU.not_equal, fill=1.0, base=2 * P,
                               pattern=[[-1, 5 * P]], channel_multiplier=1).then_inc(pool_consts, 1)
            pool.affine_select(out=eye_self[:], in_=eye_self[:], compare_op=ALU.not_equal, fill=2.0 ** (30 - 127),
                               base=0, pattern=[[-1, P]], channel_multiplier=1).then_inc(pool_consts, 1)
            pool.wait_ge(pool_consts, 1)
            rstds_of(0)
            with pool.Fori(0, U_PAIR // RING + 1) as turn:
                for s in range(RING):
                    make_lo(turn * RING + s, s)
            pool.memset(v2_hi[:].bitcast(fp32), 0.0).then_inc(v2_cleared, 1)
            pool.memset(v2_lo[:].bitcast(fp32), 0.0).then_inc(v2_cleared, 1)
            pool.wait_ge(picks_ready, 2)
            pool.tensor_tensor(picked_3, picked_3, picked_2, ALU.add).then_inc(picks_added, 1)
            with pool.Fori(U_PAIR // RING + 1, U_HEAD // RING) as turn:
                for s in range(RING):
                    make_lo(turn * RING + s, s)
            rstds_of(1)
            with pool.Fori(U_HEAD // RING, UNITS // RING) as turn:
                for s in range(RING):
                    make_lo(turn * RING + s, s)

        @block.scalar
        def _(act):
            act.wait_ge(pool_consts, 1)
            act.activation(warm[:], minus_half[:], ACT.Exp).then_inc(act_warm, 1)
            for dst, src in ((bias[:], biases), (edge[:], edge_cols),
                             (etw[:], edge_type_weights.partition_broadcast(P)),
                             (rs[:], route_scale.partition_broadcast(P))):
                act.dma_start(dst, src).then_inc(consts_landed, 16)

            def hi_at(base, step, per):
                first, turn = base
                u = first + step
                s = u % RING
                landed = 16 * (u // RING + 1)
                act.wait_ge(raw_landed[s], turn * (16 * per // RING) + landed)
                act.wait_ge(unit_used, turn * per + (u - (RING - 1)))
                act.activation(w_hi[:, s, :], w_raw[:, s, :], ACT.Copy).then_inc(hi_ready, 1)

            def hi_fixed(u, fresh=False):
                s = u % RING
                act.wait_ge(raw_landed[s], 16 * (u // RING + 1))
                if not fresh:
                    act.wait_ge(unit_used, u - (RING - 1))
                act.activation(w_hi[:, s, :], w_raw[:, s, :], ACT.Copy).then_inc(hi_ready, 1)

            def normalise(turn, t):
                act.wait_ge(rstd_ready, turn * NT + t + 1)
                act.activation(normed[:, t, :], x[:, t, :], ACT.Identity, scale=rstd[:, t:t + 1],
                               bias=shift[:, t:t + 1]).then_inc(normed_ready, 1)

            def hT_his(turn, t):
                for f in range(2):
                    n = 2 * t + f
                    act.wait_ge(normed_T, turn * LN_STEPS + n + 1)
                    act.activation(hT_hi[:, 4 * f:4 * f + 4, t * P:(t + 1) * P],
                                   bank[LN_BANKS[n]][:].rearrange("p (k n) -> p k n", k=4),
                                   ACT.Copy).then_inc(hT_hi_done, 1)

            def load_rows(piece_words):
                act.dma_start(rows[:, 0, :], src_row[piece_words].partition_broadcast(P)).then_inc(rows_landed, 16)
                act.dma_start(rows[:, 1, :], dst_row[piece_words].partition_broadcast(P)).then_inc(rows_landed, 16)

            normalise(0, 0)
            normalise(0, 1)
            hi_fixed(0, fresh=True)
            hT_his(0, 0)
            hT_his(0, 1)
            hT_his(0, 2)
            hi_fixed(1, fresh=True)
            hi_fixed(2, fresh=True)
            act.wait_ge(etw_abs_ready, 1)
            act.activation(w8[:], etw_abs[:], ACT.Exp, scale=-1.0).then_inc(etw_exp, 1)
            act.wait_ge(etw_exp1, 1)
            act.activation(etw_abs[:], w8[:], ACT.Ln).then_inc(etw_log, 1)

            with act.Fori(0, PAIRS) as j:
                for i, dst in enumerate((qT_hi, kT_hi, vT_hi)):
                    act.wait_ge(unit_used, j * 3 + i + 1)
                    act.activation(dst[:, j, :], bank[i][:, 0:N], ACT.Identity,
                                   bias=bias[:, i, bass.ds(j, 1)]).then_inc(qkv_hi_done, 1)
                    hi_at((0, j), i + 3, 3)
                act.wait_ge(keys_made, j + 1)
                load_rows(j + 1)

            def q2_hi_of(turn, b):
                act.wait_ge(unit_used, U_PAIR + 1 + turn * 3)
                act.activation(q2_hi[:], bank[6][:, 0:N], ACT.Identity, bias=b).then_inc(q2_hi_done, 1)

            def k2_hi_of(turn, b, at=6):
                act.wait_ge(unit_used, U_PAIR + 2 + turn * 3)
                act.activation(k2_hi[:], bank[at][:, 0:N], ACT.Identity, bias=b).then_inc(k2_hi_done, 1)

            def v2_hi_of(pair):
                act.wait_ge(v2_back, pair + 1)
                act.activation(v2_hi.rearrange("p t (a d) -> p t a d", a=2)[:, :, :, 0:GD],
                               bank[7][:, 0:N].rearrange("p (t a d) -> p t a d", t=NT, a=2),
                               ACT.Copy).then_inc(v2_hi_done, 1)

            def pT_hi_of(pair, head, group=None):
                banks = NT * (head if group is None else group)
                for m in range(NT):
                    act.wait_ge(probs_T, pair * 6 + NT * head + m + 1)
                    act.activation(pT_hi[:, head, m, :], bank[banks + m][:, 0:N], ACT.Copy).then_inc(pT_hi_done, 1)

            def exp_of(pair, head):
                act.wait_ge(max_ready, pair * 2 + head + 1)
                for t in range(NT):
                    c = NT * head + t
                    act.activation(S[:, c, :], S[:, c, :], ACT.Exp, bias=neg_mx[:, c:c + 1],
                                   accum_out=row_sum[:, c:c + 1]).then_inc(exp_done, 1)

            def oT_hi_of(pair, at):
                act.wait_ge(pair_out, pair + 1)
                act.activation(oT_hi[:, at, :], bank[7][:, 0:N], ACT.Copy).then_inc(oT_hi_done, 1)

            q2_hi_of(0, bias[:, 3, 0:1])
            hi_fixed(U_PAIR + 3)
            k2_hi_of(0, bias[:, 4, 0:1], 0)
            hi_fixed(U_PAIR + 4)
            exp_of(0, 0)
            exp_of(0, 1)
            with act.Fori(1, PAIRS) as j:
                hi_at((U_PAIR, j), 2, 3)
                q2_hi_of(j, bias[:, 3, bass.ds(j, 1)])
                v2_hi_of(j - 1)
                pT_hi_of(j - 1, 0)
                hi_at((U_PAIR, j), 3, 3)
                pT_hi_of(j - 1, 1)
                k2_hi_of(j, bias[:, 4, bass.ds(j, 1)])
                hi_at((U_PAIR, j), 4, 3)
                oT_hi_of(j - 1, j - 1)
                exp_of(j, 0)
                exp_of(j, 1)
            hi_fixed(U_WO + 2)
            pT_hi_of(PAIRS - 1, 0)
            v2_hi_of(PAIRS - 1)
            hi_fixed(U_WO + 3)
            pT_hi_of(PAIRS - 1, 1, 0)
            hi_fixed(U_WO + 4)
            oT_hi_of(PAIRS - 1, PAIRS - 1)
            for u in range(U_WO + 5, U_ROUTER + 2):
                hi_fixed(u)
            normalise(1, 0)
            normalise(1, 1)
            hT_his(1, 0)
            normalise(1, 2)
            hT_his(1, 1)
            hT_his(1, 2)
            hi_fixed(U_ROUTER + 2)
            act.wait_ge(unit_used, U_ROUTER + 1)
            act.activation(route[:, 0].rearrange("p g e -> p (g e)"), bank[RF][:, 0:N], ACT.Exp,
                           scale=-1.0).then_inc(router_exp, 1)

            def f_hi_of(dst, b, done, need):
                act.wait_ge(unit_used, need)
                act.activation(dst[:], bank[b][:, 0:N], ACT.Copy).then_inc(done, 1)

            def f_exp_of(head):
                for t in range(NT):
                    act.wait_ge(f_max, head * NT + t + 1)
                    act.activation(F[:, t, :], bank[SF[t]][:, 0:N], ACT.Exp, bias=neg_mx[:, t:t + 1],
                                   scale=FFN_SCALE, accum_out=row_sum[:, t:t + 1]).then_inc(f_exp, 1)

            def fv_hi_of(head):
                act.wait_ge(v_gated, head * 6 + 6)
                act.activation(v2_hi[:, :, 0:P], v_sum, ACT.Copy).then_inc(fv_hi_done, 1)

            def f_pT_hi_of(head, banks=TF):
                for m in range(NT):
                    act.wait_ge(f_probs_T, head * NT + m + 1)
                    act.activation(pT_hi[:, 0, m, :], bank[banks[m]][:, 0:N], ACT.Copy).then_inc(f_pT_hi, 1)

            def context_of(head):
                act.wait_ge(f_context, head + 1)
                act.activation(context, bank[CF][:, 0:N], ACT.Copy).then_inc(context_ready, 1)

            def gc_hi_of(head, e):
                act.wait_ge(gated_ready, head * FE + e + 1)
                act.activation(gc_hi[:, e, :], gated[:, e % 2, :], ACT.Copy).then_inc(gc_hi_done, 1)

            def load_gate_rows(head):
                act.dma_start(gate_rows,
                              gate_rows_dram[bass.ds(head * FE, FE), :].partition_broadcast(P)).then_inc(rows_ready, 16)

            hi_fixed(U_HEAD + 2)
            hi_fixed(U_HEAD + 3)
            f_hi_of(q2_hi, QF, fq_hi_done, U_HEAD + 1)
            hi_fixed(U_HEAD + 4)
            f_hi_of(k2_hi, KF, fk_hi_done, U_HEAD + 2)
            hi_fixed(U_HEAD + 5)
            hi_fixed(U_HEAD + 6)
            hi_fixed(U_HEAD + 7)
            act.wait_ge(gateT_ready, 1)
            act.dma_start(gate_rows_dram, gateT).then_inc(gates_stored, 16)
            hi_fixed(U_HEAD + 8)
            f_exp_of(0)
            hi_fixed(U_HEAD + 9)
            act.wait_ge(gates_stored, 16)
            load_gate_rows(0)
            hi_fixed(U_HEAD + 10)
            hi_fixed(U_HEAD + 11)
            hi_fixed(U_HEAD + 12)
            f_pT_hi_of(0, TF_FIRST)
            fv_hi_of(0)
            hi_fixed(U_HEAD + 13)
            f_hi_of(q2_hi, QF, fq_hi_done, U_HEAD + 11)
            f_hi_of(k2_hi, KF, fk_hi_done, U_HEAD + 12)

            def switch_head(h, last=False):
                base = (U_LOOP - BODY_UNITS, h)

                def his(first, end):
                    for i in range(first, end):
                        hi_at(base, i, BODY_UNITS)

                his(2, 3)
                context_of(h - 1)
                for e in range(4):
                    gc_hi_of(h - 1, e)
                his(3, 4)
                gc_hi_of(h - 1, 4)
                gc_hi_of(h - 1, 5)
                his(4, 5)
                gc_hi_of(h - 1, 6)
                gc_hi_of(h - 1, 7)
                load_gate_rows(h)
                his(5, 7)
                f_exp_of(h)
                his(7, 11)
                fv_hi_of(h)
                his(11, 15)
                f_pT_hi_of(h)
                if not last:
                    his(15, 20)
                    f_hi_of(q2_hi, QF, fq_hi_done, h * BODY_UNITS + (U_LOOP - BODY_UNITS + 17))
                    f_hi_of(k2_hi, KF, fk_hi_done, h * BODY_UNITS + (U_LOOP - BODY_UNITS + 18))

            with act.Fori(1, FH - 1) as h:
                switch_head(h)
            switch_head(FH - 1, last=True)
            hi_fixed(U_LAST - 1)
            hi_fixed(U_LAST)
            context_of(FH - 1)
            for e in range(4):
                gc_hi_of(FH - 1, e)
            hi_fixed(U_LAST + 1)
            hi_fixed(U_LAST + 2)
            gc_hi_of(FH - 1, 4)
            gc_hi_of(FH - 1, 5)
            hi_fixed(U_LAST + 3)
            gc_hi_of(FH - 1, 6)
            gc_hi_of(FH - 1, 7)
            for u in range(U_LAST + 4, UNITS):
                hi_fixed(u)

        @block.vector
        def _(dve):
            step = Tally(dve_step)

            def settled():
                dve.wait_ge(step.sem, step.value())

            def layer_stats(t, f):
                step.add(dve.bn_stats(stats[:, t, f, :], x[:, t, f * HALF:(f + 1) * HALF]))

            def layer_moments(t):
                settled()
                step.add(dve.bn_aggr(moments[:, t, :], stats[:, t].rearrange("p f s -> p (f s)")))
                settled()
                step.add(dve.tensor_scalar(neg_mean[:, t:t + 1], moments[:, t, 0:1], -1.0, None, ALU.mult))
                dve.tensor_scalar(var_eps[:, t:t + 1], moments[:, t, 1:2], EPS, None, ALU.add).then_inc(var_ready, 1)

            def hT_los(turn, t):
                for f in range(2):
                    n = 2 * t + f
                    dve.wait_ge(hT_hi_done, turn * LN_STEPS + n + 1)
                    to = (slice(None), slice(4 * f, 4 * f + 4), slice(t * P, (t + 1) * P))
                    dve.tensor_tensor(hT_lo[to], bank[LN_BANKS[n]][:].rearrange("p (k n) -> p k n", k=4),
                                      hT_hi[to].bitcast(fp32), ALU.subtract).then_inc(hT_lo_done, 1)

            dve.wait_ge(x0_landed, 16)
            layer_stats(0, 0)
            for t in range(NT):
                dve.wait_ge(x_landed[t], 16)
                for f in range(0 if t else 1, 2):
                    layer_stats(t, f)
                layer_moments(t)
            dve.wait_ge(consts_landed, 16 * 4)
            dve.scalar_tensor_tensor(etw_abs[:], etw[:], -1.0, etw[:], ALU.mult, ALU.max).then_inc(etw_abs_ready, 1)
            dve.wait_ge(rstd_ready, NT)
            dve.tensor_scalar(normed[:, NT - 1, :], x[:, NT - 1, :], moments[:, NT - 1, 0:1], rstd[:, NT - 1:NT],
                              ALU.subtract, ALU.mult).then_inc(last_normed, 1)
            for t in range(NT):
                hT_los(0, t)
            dve.wait_ge(pool_consts, 15)
            step.add(dve.tensor_copy(iota[:], iota_i))
            step.add(dve.tensor_copy(table[:, :, 1], edge[:, 0, :]))
            step.add(dve.tensor_copy(table[:, :, 2], edge[:, 1, :]))
            step.add(dve.tensor_scalar(code[:], edge[:, 2, :], 3.0, None, ALU.add))
            settled()
            step.add(dve.scalar_tensor_tensor(table[:, :, 0], table[:, :, 1], float(N), table[:, :, 2], ALU.mult,
                                              ALU.add))
            step.add(dve.tensor_scalar(code[:], code[:], 3, None, ALU.bitwise_and))
            settled()
            step.add(dve.tensor_tensor(code[:], code[:], chunk_base[:], ALU.add))
            settled()
            step.add(dve.tensor_scalar(code[:], code[:], 23, None, ALU.logical_shift_left))
            settled()
            step.add(dve.tensor_copy(table[:, :, 3], code[:].bitcast(fp32)))
            dve.wait_ge(etw_exp, 1)
            dve.tensor_scalar(w8[:], w8[:], 1.0, None, ALU.add).then_inc(etw_exp1, 1)
            dve.wait_ge(bo_landed, 16)
            dve.wait_ge(normed_ready, NT - 1)
            dve.wait_ge(last_normed, 1)

            def qkv_lo_of(j, i, dst, hi):
                dve.wait_ge(qkv_hi_done, j * 3 + i + 1)
                dve.scalar_tensor_tensor(dst[:, j, :], bank[i][:, 0:N], bias[:, i, bass.ds(j, 1)],
                                         hi[:, j, :].bitcast(fp32), ALU.add, ALU.subtract).then_inc(qkv_lo_done, 1)

            settled()
            with dve.Fori(0, PAIRS) as j:
                step.enter(j, 5)
                dve.wait_ge(rows_landed, j * 32 + 32)
                dve.scalar_tensor_tensor(keys.rearrange("p c q -> p (c q)"), rows[:, 0, :], float(N), rows[:, 1, :],
                                         ALU.mult, ALU.add).then_inc(keys_made, 1)
                step.add(dve.tensor_copy(now[:], table[:, bass.ds(j * PIECE, PIECE), :]))
                settled()
                dve.wait_ge(keys_made, j + 1)
                step.add(dve.tensor_tensor(keys, keys, now[:, :, 0:1].to_broadcast([P, PIECE, P]), ALU.is_equal))
                settled()
                step.add(dve.tensor_tensor(keys, keys, later[:].unsqueeze(1).to_broadcast([P, PIECE, P]), ALU.mult))
                settled()
                step.add(dve.tensor_reduce(dup[:], keys, AX, ALU.max))
                settled()
                step.add(dve.scalar_tensor_tensor(weight[:], dup[:], 0.0, now[:, :, 3], ALU.is_equal, ALU.mult))
                settled()
                qkv_lo_of(j, 0, qT_lo, qT_hi)
                dve.wait_ge(hot_used, j + 1)
                for c in range(PIECE):
                    dve.tensor_scalar(hot[:, 0, c, :], iota[:], now[:, c, 1:2], weight[:, c:c + 1], ALU.is_equal,
                                      ALU.mult).then_inc(hot_ready, 1)
                    dve.tensor_scalar(hot[:, 1, c, :], iota[:], now[:, c, 2:3], None,
                                      ALU.is_equal).then_inc(hot_ready, 1)
                qkv_lo_of(j, 1, kT_lo, kT_hi)
                qkv_lo_of(j, 2, vT_lo, vT_hi)
                of_j = bass.ds(j * P, P)
                dve.tensor_tensor(x[:, :, of_j], x[:, :, of_j],
                                  bo_row[:, of_j].unsqueeze(1).to_broadcast([P, NT, P]), ALU.add).then_inc(bo_added, 1)
                dve.wait_ge(hot_ready, j * (2 * PIECE) + 2 * PIECE)
            step.leave(PAIRS)
            dve.wait_ge(bo_added, PAIRS)
            dve.wait_ge(etw_log, 1)
            step.add(dve.scalar_tensor_tensor(w8[:], etw[:], 0.0, etw_abs[:], ALU.max, ALU.add))
            settled()
            step.add(dve.tensor_scalar(w8[:], w8[:], 8.0, None, ALU.mult))

            def split_lo(dst, src, hi, b, done):
                if b is None:
                    dve.tensor_tensor(dst, src, hi.bitcast(fp32), ALU.subtract).then_inc(done, 1)
                else:
                    dve.scalar_tensor_tensor(dst, src, b, hi.bitcast(fp32), ALU.add, ALU.subtract).then_inc(done, 1)

            def v2_lo_of(pair):
                dve.wait_ge(v2_hi_done, pair + 1)
                split_lo(v2_lo.rearrange("p t (a d) -> p t a d", a=2)[:, :, :, 0:GD],
                         bank[7][:, 0:N].rearrange("p (t a d) -> p t a d", t=NT, a=2),
                         v2_hi.rearrange("p t (a d) -> p t a d", a=2)[:, :, :, 0:GD], None, v2_lo_done)

            def pT_lo_of(pair, head, group=None):
                banks = NT * (head if group is None else group)
                for m in range(NT):
                    dve.wait_ge(pT_hi_done, pair * 6 + NT * head + m + 1)
                    split_lo(pT_lo[:, head, m, :], bank[banks + m][:, 0:N], pT_hi[:, head, m, :], None, pT_lo_done)

            def max_of(pair, head):
                for t in range(NT):
                    c = NT * head + t
                    dve.wait_ge(scores_done, pair * 6 + 2 * t + head + 1)
                    step.add(dve.memset(holds[:, c:c + 1], 0.0))
                    dve.wait_ge(mask_ready, 1)
                    step.add(dve.tensor_tensor_reduce(S[:, c, :], bank[c][:, 0:N], mask8[:, t, :], scale=GNN_SCALE,
                                                      scalar=-3e38, op0=ALU.add, op1=ALU.max,
                                                      accum_out=mx[:, c:c + 1]))
                settled()
                dve.tensor_scalar(neg_mx[:, NT * head:NT * head + NT], mx[:, NT * head:NT * head + NT], -1.0, None,
                                  ALU.mult).then_inc(max_ready, 1)

            def norm_of(pair, head):
                cs = slice(NT * head, NT * head + NT)
                dve.wait_ge(exp_done, pair * 6 + NT * head + NT)
                step.add(dve.reciprocal(inv_sum[:, cs], row_sum[:, cs]))
                settled()
                for c in range(NT * head, NT * head + NT):
                    dve.tensor_scalar(S[:, c, :], S[:, c, :], inv_sum[:, c:c + 1], None,
                                      ALU.mult).then_inc(norm_done, 1)

            def v2T_of(pair, b):
                dve.wait_ge(unit_used, pair * 3 + (U_PAIR + 3))
                dve.tensor_scalar(v2T, bank[7][:, 0:N], b, None, ALU.add).then_inc(v2T_ready, 1)

            def q2_lo_of(pair, b):
                dve.wait_ge(q2_hi_done, pair + 1)
                split_lo(q2_lo[:], bank[6][:, 0:N], q2_hi[:], b, q2_lo_done)

            def k2_lo_of(pair, b, at=6):
                dve.wait_ge(k2_hi_done, pair + 1)
                split_lo(k2_lo[:], bank[at][:, 0:N], k2_hi[:], b, k2_lo_done)

            def oT_lo_of(pair, at):
                dve.wait_ge(oT_hi_done, pair + 1)
                split_lo(oT_lo[:, at, :], bank[7][:, 0:N], oT_hi[:, at, :], None, oT_lo_done)

            dve.wait_ge(rows_landed, 32 * (PAIRS + 1))
            dve.wait_ge(counts_done, 1)
            for t in range(NT):
                step.add(dve.tensor_copy(counts[:, t, :], bank[3 + t][:, 0:N]))
            settled()
            flat = counts.rearrange("p t n -> p (t n)")
            mask_flat = mask8[:].rearrange("p t n -> p (t n)")
            step.add(dve.tensor_scalar(types, flat.bitcast(int32), 23, 3, ALU.logical_shift_right, ALU.bitwise_and))
            settled()
            for k, dst in ((3, picked_3), (2, picked_2)):
                dve.tensor_scalar(dst, types, float(k), w8[:, k:k + 1], ALU.is_equal, ALU.mult).then_inc(picks_ready, 1)
            step.add(dve.tensor_scalar(mask_flat, flat, 0.0, NO_EDGE, ALU.is_equal, ALU.mult))
            q2_lo_of(0, bias[:, 3, 0:1])
            for k in (0, 1):
                step.add(dve.tensor_scalar(picked, types, float(k), w8[:, k:k + 1], ALU.is_equal, ALU.mult))
                settled()
                step.add(dve.tensor_tensor(mask_flat, mask_flat, picked, ALU.add))
                settled()
            k2_lo_of(0, bias[:, 4, 0:1], 0)
            dve.wait_ge(picks_added, 1)
            last = dve.tensor_tensor(mask_flat, mask_flat, picked_3, ALU.add)
            last.then_inc(mask_ready, 1)
            v2T_of(0, bias[:, 5, 0:1])
            max_of(0, 0)
            max_of(0, 1)
            norm_of(0, 0)
            norm_of(0, 1)
            with dve.Fori(1, PAIRS) as j:
                step.enter(j - 1, 14)
                q2_lo_of(j, bias[:, 3, bass.ds(j, 1)])
                v2_lo_of(j - 1)
                pT_lo_of(j - 1, 0)
                pT_lo_of(j - 1, 1)
                k2_lo_of(j, bias[:, 4, bass.ds(j, 1)])
                oT_lo_of(j - 1, j - 1)
                max_of(j, 0)
                max_of(j, 1)
                norm_of(j, 0)
                norm_of(j, 1)
                v2T_of(j, bias[:, 5, bass.ds(j, 1)])
            step.leave(PAIRS - 1)
            pT_lo_of(PAIRS - 1, 0)
            v2_lo_of(PAIRS - 1)
            pT_lo_of(PAIRS - 1, 1, 0)
            oT_lo_of(PAIRS - 1, PAIRS - 1)

            def add_gnn(f, t):
                dve.tensor_tensor(x[:, t, f * HALF:(f + 1) * HALF], bank[WO_BANKS[f][t]][:, 0:HALF],
                                  x[:, t, f * HALF:(f + 1) * HALF], ALU.add).then_inc(out_added, 1)

            dve.wait_ge(unit_used, U_WO + 4)
            for t in range(NT):
                add_gnn(0, t)
            dve.wait_ge(out_added, NT)
            for t in range(NT):
                layer_stats(t, 0)
            for t in range(NT):
                if t < NT - 1:
                    dve.wait_ge(tile_done, t + 1)
                else:
                    dve.wait_ge(unit_used, U_WO + 8)
                add_gnn(1, t)
                dve.wait_ge(out_added, NT + t + 1)
                layer_stats(t, 1)
                layer_moments(t)
            for t in range(NT):
                hT_los(1, t)

            G = NT * GROUPS
            probs, ranked, pick1, rest, pick2 = (route[:, a] for a in range(5))
            top1, top2, rank, total, scale1, scale2 = (best[:, a, :] for a in range(6))

            def spread(a):
                return a.unsqueeze(2).to_broadcast([P, G, FE])

            dve.wait_ge(router_exp, 1)
            step.add(dve.tensor_scalar(ranked, probs, 1.0, None, ALU.add))
            settled()
            step.add(dve.reciprocal(probs, ranked))
            settled()
            for left, top, pick in ((probs, top1, pick1), (rest, top2, pick2)):
                step.add(dve.tensor_reduce(top, left, AX, ALU.max))
                settled()
                step.add(dve.tensor_tensor(ranked, left, spread(top), ALU.is_equal))
                settled()
                step.add(dve.tensor_tensor(ranked, ranked, desc[:].unsqueeze(1).to_broadcast([P, G, FE]), ALU.mult))
                settled()
                step.add(dve.tensor_reduce(rank, ranked, AX, ALU.max))
                settled()
                step.add(dve.tensor_tensor(pick, ranked, spread(rank), ALU.is_equal))
                settled()
                if pick is pick1:
                    step.add(dve.scalar_tensor_tensor(rest.rearrange("p g e -> p (g e)"),
                                                      pick1.rearrange("p g e -> p (g e)"), -2.0,
                                                      probs.rearrange("p g e -> p (g e)"), ALU.mult, ALU.add))
                    settled()
            step.add(dve.tensor_tensor(total, top1, top2, ALU.add))
            settled()
            step.add(dve.tensor_scalar(total, total, 1e-9, None, ALU.max))
            settled()
            step.add(dve.reciprocal(rank, total))
            settled()
            step.add(dve.tensor_tensor(scale1, top1, rank, ALU.mult))
            step.add(dve.tensor_tensor(scale2, top2, rank, ALU.mult))
            settled()
            step.add(dve.tensor_scalar(best[:, 4:6, :], best[:, 4:6, :], rs[:, 0:1], None, ALU.mult))
            settled()
            step.add(dve.tensor_tensor(pick1, pick1, spread(scale1), ALU.mult))
            step.add(dve.tensor_tensor(pick2, pick2, spread(scale2), ALU.mult))
            settled()
            dve.tensor_tensor(gates.rearrange("p t (g e) -> p (t g) e", e=FE), pick1, pick2,
                              ALU.add).then_inc(gates_ready, 1)

            def f_lo_of(dst, hi, b, hi_done, lo_done, head):
                dve.wait_ge(hi_done, head + 1)
                split_lo(dst[:], bank[b][:, 0:N], hi[:], None, lo_done)

            def gate_copy(head):
                step.add(dve.tensor_copy(v_gate[:], gates[:, :, bass.ds(head * FE, FE)]))

            def gate_values(head, g, need):
                dve.wait_ge(unit_used, need)
                for ts in ((0,), (1, 2)):
                    for e in range(4):
                        settled()
                        for t in ts:
                            src = bank[VF[g][t]][:, e * P:(e + 1) * P]
                            col = v_gate[:, t, 4 * g + e:4 * g + e + 1]
                            if g == 0 and e == 0:
                                ins = dve.tensor_scalar(v_sum[:, t, :], src, col, None, ALU.mult)
                            else:
                                ins = dve.scalar_tensor_tensor(v_sum[:, t, :], src, col, v_sum[:, t, :], ALU.mult,
                                                               ALU.add)
                            if e < 3:
                                step.add(ins)
                            else:
                                ins.then_inc(v_gated, 1)
                dve.wait_ge(v_gated, head * 6 + 3 * g + 3)

            def f_max_of(head):
                for t in range(NT):
                    dve.wait_ge(f_scores, head * NT + t + 1)
                    step.add(dve.tensor_reduce(mx[:, t:t + 1], bank[SF[t]][:, 0:N], AX, ALU.max))
                    settled()
                    dve.tensor_scalar(neg_mx[:, t:t + 1], mx[:, t:t + 1], -FFN_SCALE, None,
                                      ALU.mult).then_inc(f_max, 1)

            def f_norm_of(head):
                dve.wait_ge(f_exp, head * NT + NT)
                step.add(dve.reciprocal(inv_sum[:, 0:NT], row_sum[:, 0:NT]))
                settled()
                for t in range(NT):
                    dve.tensor_scalar(F[:, t, :], F[:, t, :], inv_sum[:, t:t + 1], None,
                                      ALU.mult).then_inc(f_norm, 1)

            def fv_lo_of(head):
                dve.wait_ge(fv_hi_done, head + 1)
                split_lo(v2_lo[:, :, 0:P], v_sum, v2_hi[:, :, 0:P], None, fv_lo_done)

            def f_pT_lo_of(head, banks=TF):
                for m in range(NT):
                    dve.wait_ge(f_pT_hi, head * NT + m + 1)
                    split_lo(pT_lo[:, 0, m, :], bank[banks[m]][:, 0:N], pT_hi[:, 0, m, :], None, f_pT_lo)

            def gate_context(head, e):
                if e == 0:
                    dve.wait_ge(context_ready, head + 1)
                    dve.wait_ge(rows_ready, head * 16 + 16)
                if e >= 2:
                    dve.wait_ge(gc_lo_done, head * FE + e - 1)
                dve.tensor_tensor(gated[:, e % 2, :], context, gate_rows[:, e, :], ALU.mult).then_inc(gated_ready, 1)

            def gc_lo_of(head, e):
                dve.wait_ge(gc_hi_done, head * FE + e + 1)
                split_lo(gc_lo[:, e, :], gated[:, e % 2, :], gc_hi[:, e, :], None, gc_lo_done)

            def gate_contexts(head, first=0, end=FE):
                if first == 0:
                    gate_context(head, 0)
                for e in range(first, end):
                    if e + 1 < FE:
                        gate_context(head, e + 1)
                    gc_lo_of(head, e)

            def add_out_tile(f, t, banks):
                dve.tensor_tensor(x[:, t, f * HALF:(f + 1) * HALF], bank[banks[t]][:, 0:HALF],
                                  x[:, t, f * HALF:(f + 1) * HALF], ALU.add).then_inc(out_added, 1)

            def add_out(f, need, banks):
                dve.wait_ge(unit_used, need)
                for t in range(NT):
                    add_out_tile(f, t, banks)

            dve.wait_ge(gates_ready, 1)
            gate_copy(0)
            f_lo_of(q2_lo, q2_hi, QF, fq_hi_done, fq_lo_done, 0)
            f_lo_of(k2_lo, k2_hi, KF, fk_hi_done, fk_lo_done, 0)
            dve.wait_ge(gates_T, 1)
            dve.tensor_copy(gateT, bank[GF][0:FH * FE, 0:N]).then_inc(gateT_ready, 1)
            gate_values(0, 0, U_HEAD + 6)
            f_max_of(0)
            f_norm_of(0)
            gate_values(0, 1, U_HEAD + 10)
            f_pT_lo_of(0, TF_FIRST)
            fv_lo_of(0)
            f_lo_of(q2_lo, q2_hi, QF, fq_hi_done, fq_lo_done, 1)
            f_lo_of(k2_lo, k2_hi, KF, fk_hi_done, fk_lo_done, 1)

            def switch_head(h, last=False):
                u = h * BODY_UNITS + (U_LOOP - BODY_UNITS)
                gate_copy(h)
                gate_contexts(h - 1)
                gate_values(h, 0, u + 4)
                f_max_of(h)
                f_norm_of(h)
                gate_values(h, 1, u + 8)
                fv_lo_of(h)
                dve.wait_ge(out_added, h * 6)
                add_out(0, u + 12, OF[0])
                f_pT_lo_of(h)
                if not last:
                    add_out(1, u + 16, OF[1])
                    f_lo_of(q2_lo, q2_hi, QF, fq_hi_done, fq_lo_done, h + 1)
                    f_lo_of(k2_lo, k2_hi, KF, fk_hi_done, fk_lo_done, h + 1)

            with dve.Fori(1, FH - 1) as h:
                step.enter(h - 1, 1 + 18 + 3 + 1)
                switch_head(h)
            step.leave(FH - 2)
            switch_head(FH - 1, last=True)
            gate_contexts(FH - 1, 0, 4)
            add_out(1, U_LAST, OF[1])
            gate_contexts(FH - 1, 4)
            dve.wait_ge(out_added, FH * 6)
            add_out(0, U_LAST + 4, OF_LAST[0])
            for t in range(NT):
                if t < NT - 1:
                    dve.wait_ge(tile_done, NT - 1 + t + 1)
                else:
                    dve.wait_ge(unit_used, UNITS)
                add_out_tile(1, t, OF_LAST[1])

        @block.tensor
        def _(pe):
            def three(dst, a_hi, a_lo, b_hi, b_lo, first, last):
                pe.matmul(dst, a_hi, b_hi, start=first, stop=False)
                pe.matmul(dst, a_hi, b_lo, start=False, stop=False)
                return pe.matmul(dst, a_lo, b_hi, start=False, stop=last)

            def column_unit(u, s, dst, b_hi, b_lo):
                pe.wait_ge(lo_ready, u + 1)
                for k in range(KT):
                    c = slice(k * P, (k + 1) * P)
                    last = three(dst[:, 0:N], w_hi[:, s, c], w_lo[:, s, c], b_hi[:, k, :], b_lo[:, k, :], k == 0,
                                 k == KT - 1)
                last.then_inc(unit_used, 1)

            def row_unit(u, s, banks, a_hi, a_lo, i, third=None, second_half=None):
                pe.wait_ge(lo_ready, u + 1)
                for kk in range(2):
                    c = slice(kk * HALF, (kk + 1) * HALF)
                    if kk and second_half:
                        pe.wait_ge(*second_half)
                    for t in range(NT):
                        tok = slice(t * P, (t + 1) * P)
                        k = 2 * i + kk
                        if third and t == 2 and k == 0:
                            pe.wait_ge(*third)
                        last = three(bank[banks[t]][:, 0:HALF], a_hi[:, k, tok], a_lo[:, k, tok], w_hi[:, s, c],
                                     w_lo[:, s, c], k == 0, k == KT - 1)
                last.then_inc(unit_used, 1)

            def closing_row_unit(u, s, banks, a_hi, a_lo):
                pe.wait_ge(lo_ready, u + 1)
                for t in range(NT):
                    tok = slice(t * P, (t + 1) * P)
                    for kk in range(2):
                        c = slice(kk * HALF, (kk + 1) * HALF)
                        k = 6 + kk
                        last = three(bank[banks[t]][:, 0:HALF], a_hi[:, k, tok], a_lo[:, k, tok], w_hi[:, s, c],
                                     w_lo[:, s, c], False, k == KT - 1)
                    last.then_inc(unit_used if t == NT - 1 else tile_done, 1)

            def turn(dst, src):
                return pe.transpose(dst, src, ident[:])

            def normed_turns(turns, t):
                if turns == 0 and t == NT - 1:
                    pe.wait_ge(last_normed, 1)
                else:
                    pe.wait_ge(normed_ready, turns * (NT - 1) + t + 1)
                for f in range(2):
                    n = 2 * t + f
                    for kk in range(4):
                        k = 4 * f + kk
                        last = turn(bank[LN_BANKS[n]][:, kk * P:(kk + 1) * P], normed[:, t, k * P:(k + 1) * P])
                    last.then_inc(normed_T, 1)

            pe.wait_ge(pool_consts, 15)
            for t in range(NT):
                normed_turns(0, t)
            pe.wait_ge(hT_lo_done, LN_STEPS)

            def self_edges(first):
                for t in range(NT):
                    last = pe.matmul(bank[3 + t][:, 0:N], eye_self[:],
                                     eye_wide[:, (2 - t) * P:(5 - t) * P], start=first, stop=not first)
                return last

            self_edges(True).then_inc(hot_used, 1)
            with pe.Fori(0, PAIRS) as j:
                for i in range(3):
                    column_unit(j * 3 + i, i, bank[i], hT_hi, hT_lo)
                for c in range(PIECE):
                    pe.wait_ge(hot_ready, j * (2 * PIECE) + 2 * c + 2)
                    for t in range(NT):
                        last = pe.matmul(bank[3 + t][:, 0:N], hot[:, 0, c, t * P:(t + 1) * P], hot[:, 1, c, :],
                                         start=False, stop=False)
                last.then_inc(hot_used, 1)
                pe.wait_ge(qkv_lo_done, j * 3 + 3)
            self_edges(False).then_inc(counts_done, 1)

            def scores_of(pair):
                pe.wait_ge(q2_lo_done, pair + 1)
                pe.wait_ge(k2_lo_done, pair + 1)
                for t in range(NT):
                    tok = slice(t * P, (t + 1) * P)
                    for n, (a, b) in enumerate(((q2_hi, k2_hi), (q2_hi, k2_lo), (q2_lo, k2_hi))):
                        for head in range(2):
                            p = slice(GD * head, GD * head + GD)
                            last = pe.matmul(bank[NT * head + t][:, 0:N], a[p, tok], b[p, :], start=n == 0,
                                             stop=n == 2)
                            if n == 2:
                                last.then_inc(scores_done, 1)

            def probs_of(pair, head, group=None):
                banks = NT * (head if group is None else group)
                pe.wait_ge(norm_done, pair * 6 + NT * head + NT)
                for m in range(NT):
                    for t in range(NT):
                        last = turn(bank[banks + m][:, t * P:(t + 1) * P],
                                    S[:, NT * head + t, m * P:(m + 1) * P])
                    last.then_inc(probs_T, 1)

            def values_back(pair):
                pe.wait_ge(v2T_ready, pair + 1)
                for t in range(NT):
                    last = turn(bank[7][:, t * P:(t + 1) * P], v2T[:, t * P:(t + 1) * P])
                last.then_inc(v2_back, 1)

            def attend(pair):
                pe.wait_ge(v2_lo_done, pair + 1)
                pe.wait_ge(pT_lo_done, pair * 6 + 6)
                for head in range(2):
                    c = slice(GD * head, GD * head + P)
                    for m in range(NT):
                        last = three(bank[7][:, 0:N], v2_hi[:, m, c], v2_lo[:, m, c], pT_hi[:, head, m, :],
                                     pT_lo[:, head, m, :], head == 0 and m == 0, head == 1 and m == NT - 1)
                last.then_inc(pair_out, 1)

            column_unit(U_PAIR, 0, bank[6], qT_hi, qT_lo)
            column_unit(U_PAIR + 1, 1, bank[0], kT_hi, kT_lo)
            column_unit(U_PAIR + 2, 2, bank[7], vT_hi, vT_lo)
            scores_of(0)
            pe.wait_ge(v2_cleared, 2)
            with pe.Fori(1, PAIRS) as j:
                pe.wait_ge(k2_lo_done, j)
                column_unit(j * 3 + U_PAIR, 0, bank[6], qT_hi, qT_lo)
                values_back(j - 1)
                probs_of(j - 1, 0)
                probs_of(j - 1, 1)
                pe.wait_ge(q2_lo_done, j + 1)
                column_unit(j * 3 + (U_PAIR + 1), 1, bank[6], kT_hi, kT_lo)
                attend(j - 1)
                scores_of(j)
                pe.wait_ge(oT_lo_done, j)
                column_unit(j * 3 + (U_PAIR + 2), 2, bank[7], vT_hi, vT_lo)
            def project(n, second_half=None):
                row_unit(U_WO + n, (U_WO + n) % RING, WO_BANKS[n // 4], oT_hi, oT_lo, n % 4,
                         second_half=second_half)

            pe.wait_ge(max_ready, PAIRS * 2)
            project(0)
            probs_of(PAIRS - 1, 0)
            values_back(PAIRS - 1)
            project(1)
            pe.wait_ge(pT_lo_done, PAIRS * 6 - NT)
            probs_of(PAIRS - 1, 1, 0)
            project(2)
            attend(PAIRS - 1)
            project(3, (oT_lo_done, PAIRS))
            for n in range(4, 7):
                project(n)
            closing_row_unit(U_WO + 7, (U_WO + 7) % RING, WO_BANKS[1], oT_hi, oT_lo)

            def router(t):
                pe.wait_ge(hT_lo_done, LN_STEPS + 2 * t + 2)
                tok = slice(t * P, (t + 1) * P)
                for k in range(KT):
                    c = slice(k * P, (k + 1) * P)
                    s = U_ROUTER % RING
                    last = three(bank[RF][:, tok], hT_hi[:, k, tok], hT_lo[:, k, tok], w_hi[:, s, c], w_lo[:, s, c],
                                 k == 0, k == KT - 1)
                return last

            normed_turns(1, 0)
            normed_turns(1, 1)
            normed_turns(1, 2)
            pe.wait_ge(lo_ready, U_ROUTER + 1)
            pe.wait_ge(out_added, 2 * NT)
            router(0)
            router(1)
            router(2).then_inc(unit_used, 1)

            def values_units(head, g, u, s, experts=range(4), third=None):
                if g:
                    third = (v_gated, head * 6 + 1)
                for i in experts:
                    row_unit(u + 4 * g + i, (s + 4 * g + i) % RING, VF[g], hT_hi, hT_lo, i, third)

            def f_scores_of(head):
                pe.wait_ge(fq_lo_done, head + 1)
                pe.wait_ge(fk_lo_done, head + 1)
                for t in range(NT):
                    tok = slice(t * P, (t + 1) * P)
                    three(bank[SF[t]][:, 0:N], q2_hi[:, tok], q2_lo[:, tok], k2_hi[:], k2_lo[:], True,
                          True).then_inc(f_scores, 1)

            def f_probs_of(head, banks=TF):
                pe.wait_ge(f_norm, head * NT + NT)
                for m in range(NT):
                    for t in range(NT):
                        last = turn(bank[banks[m]][:, t * P:(t + 1) * P], F[:, t, m * P:(m + 1) * P])
                    last.then_inc(f_probs_T, 1)

            def f_attend(head):
                pe.wait_ge(fv_lo_done, head + 1)
                for m in range(NT):
                    pe.wait_ge(f_pT_lo, head * NT + m + 1)
                    last = three(bank[CF][:, 0:N], v2_hi[:, m, 0:P],
                                 v2_lo[:, m, 0:P], pT_hi[:, 0, m, :], pT_lo[:, 0, m, :], m == 0, m == NT - 1)
                last.then_inc(f_context, 1)

            def output_units(head, f, u, s, parts=range(4)):
                for i in parts:
                    row_unit(u + i, (s + i) % RING, OF[f], gc_hi, gc_lo, i,
                             (out_added, head * 6 + 7) if f else None)

            column_unit(U_HEAD, U_HEAD % RING, bank[QF], hT_hi, hT_lo)
            column_unit(U_HEAD + 1, (U_HEAD + 1) % RING, bank[KF], hT_hi, hT_lo)
            pe.wait_ge(router_exp, 1)
            values_units(0, 0, U_HEAD + 2, (U_HEAD + 2) % RING, range(3))
            pe.wait_ge(gates_ready, 1)
            for t in range(NT):
                last = turn(bank[GF][0:FH * FE, t * P:(t + 1) * P], gates[:, t, FH * FE:2 * FH * FE])
            last.then_inc(gates_T, 1)
            values_units(0, 0, U_HEAD + 2, (U_HEAD + 2) % RING, (3,))
            pe.wait_ge(gateT_ready, 1)
            f_scores_of(0)
            values_units(0, 1, U_HEAD + 2, (U_HEAD + 2) % RING)
            pe.wait_ge(v_gated, NT)
            f_probs_of(0, TF_FIRST)
            column_unit(U_HEAD + 10, (U_HEAD + 10) % RING, bank[QF], hT_hi, hT_lo)
            pe.wait_ge(v_gated, 2 * NT)
            column_unit(U_HEAD + 11, (U_HEAD + 11) % RING, bank[KF], hT_hi, hT_lo)
            pe.wait_ge(f_pT_lo, NT)
            f_attend(0)

            def switch_head(h, last=False):
                u = h * BODY_UNITS + (U_LOOP - BODY_UNITS)
                s = U_LOOP % RING
                pe.wait_ge(out_added, h * 6)
                values_units(h, 0, u, s, third=(context_ready, h))
                f_scores_of(h)
                values_units(h, 1, u, s)
                pe.wait_ge(v_gated, h * 6 + 3)
                pe.wait_ge(f_exp, h * NT + NT)
                pe.wait_ge(gc_lo_done, h * FE)
                output_units(h - 1, 0, u + 8, s + 8)
                pe.wait_ge(v_gated, h * 6 + 6)
                f_probs_of(h)
                output_units(h - 1, 1, u + 12, s + 12, range(2) if last else range(4))
                if not last:
                    pe.wait_ge(out_added, h * 6 + 3)
                    column_unit(u + 16, (s + 16) % RING, bank[QF], hT_hi, hT_lo)
                    pe.wait_ge(f_pT_lo, h * NT + NT)
                    column_unit(u + 17, (s + 17) % RING, bank[KF], hT_hi, hT_lo)
                pe.wait_ge(out_added, h * 6 + 2)
                f_attend(h)
                if last:
                    output_units(h - 1, 1, u + 12, s + 12, range(2, 4))

            with pe.Fori(1, FH - 1) as h:
                switch_head(h)
            switch_head(FH - 1, last=True)
            for n in range(8):
                f, i = n // 4, n % 4
                u = U_LAST + n
                if f == 0:
                    pe.wait_ge(gc_lo_done, (FH - 1) * FE + 2 * i + 2)
                if n == 4:
                    pe.wait_ge(out_added, FH * 6)
                if n < 7:
                    row_unit(u, u % RING, OF_LAST[f], gc_hi, gc_lo, i)
                else:
                    closing_row_unit(u, u % RING, OF_LAST[f], gc_hi, gc_lo)


def kernel(**inputs):
    import numpy as np
    import concourse.bacc as bacc
    from concourse.bass_utils import run_bass_kernel_spmd

    a = {name: np.asarray(value) for name, value in inputs.items()}
    g = {name[len("L0_gnn_"):]: v for name, v in a.items() if name.startswith("L0_gnn_")}
    f = {name[len("L0_ffn_"):]: v for name, v in a.items() if name.startswith("L0_ffn_")}

    def column_units(w):
        o = w.shape[0] // P
        return w.reshape(o, P, KT, P).transpose(0, 3, 2, 1).reshape(o, P, D)

    def row_units(w):
        o = w.shape[1] // HALF
        return w.reshape(4, 2, P, o, HALF).transpose(3, 0, 2, 1, 4).reshape(o * 4, P, D)

    def by_turns(*lots):
        return np.stack(lots, axis=1).reshape(-1, P, D)

    q, k = column_units(f["q_w"]), column_units(f["k_w"])
    v_w = f["v_w"].reshape(FH, FE, D, P).transpose(0, 2, 1, 3).reshape(FH, D, FE * P)
    o_w = f["o_w"].reshape(FH, FE * P, D)
    lots = [by_turns(*(column_units(g[n]) for n in ("wq", "wk", "wv"))),
            by_turns(*(column_units(g[n]) for n in ("wiq", "wik", "wiv"))),
            row_units(g["wo"].T),
            column_units(np.concatenate([f["sel_v_w"], f["sel_o_w"]]))]
    lots += [q[:1], k[:1]]
    for h in range(FH):
        lots.append(row_units(v_w[h]))
        if h:
            lots.append(row_units(o_w[h - 1]))
        if h < FH - 1:
            lots += [q[h + 1:h + 2], k[h + 1:h + 2]]
    lots.append(row_units(o_w[FH - 1]))
    arrays = {
        "x": a["x"],
        "units": np.concatenate(lots),
        "biases": np.stack([g[n].reshape(KT, P).T for n in ("bq", "bk", "bv", "biq", "bik", "biv")], axis=1),
        "bo": g["bo"],
        "edge_type_weights": g["edge_type_weights"],
        "route_scale": f["route_scale"],
        "edge_cols": np.stack([a[n].reshape(CHUNKS, P).T for n in ("src", "dst", "edge_type_5")], axis=1),
        "src_row": np.concatenate([a["src"], a["src"][:PIECE * P]]).reshape(PAIRS + 1, PIECE * P),
        "dst_row": np.concatenate([a["dst"], a["dst"][:PIECE * P]]).reshape(PAIRS + 1, PIECE * P),
    }
    assert arrays["units"].shape == (UNITS, P, D)
    arrays = {name: np.ascontiguousarray(v) for name, v in arrays.items()}
    nc = bacc.Bacc("TRN2", target_bir_lowering=False, num_devices=1)
    args = [nc.dram_tensor(f"in_{name}", v.shape, mybir.dt.from_np(v.dtype), kind="ExternalInput").ap()
            for name, v in arrays.items()]
    out = nc.dram_tensor("out_x", (N, D), mybir.dt.float32, kind="ExternalOutput").ap()
    gnn_switch_kernel(nc, *args, out)
    result = run_bass_kernel_spmd(nc, [{f"in_{name}": v for name, v in arrays.items()}], core_ids=[0])
    return result.results[0]["out_x"]
```
